# Optimizing a Trainium2 kernel written in Bass

```python
import numpy as np
import jax
import jax.numpy as jnp

def _softmax(x, axis=-1):
    return jax.nn.softmax(x, axis=axis)

def _gelu(x):
    return jax.nn.gelu(x, approximate=True)

def _silu(x):
    return jax.nn.silu(x)

def _sigmoid(x):
    return jax.nn.sigmoid(x)

def _layernorm(x, axis=-1, eps=1e-05):
    m = jnp.mean(x, axis=axis, keepdims=True)
    v = jnp.var(x, axis=axis, keepdims=True)
    return (x - m) / jnp.sqrt(v + eps)

def _scatter_add(tgt, idx, src, axis=0):
    return tgt.at[idx].add(src)

def _segment_sum(src, seg, n):
    return jax.ops.segment_sum(src, seg, n)
kernel_name = 'mk_flamingo_gated_d2_seqx_r8_a1b2dc'

def setup_inputs(seed: int=0):
    np.random.seed(seed)
    _w = jnp.asarray

    def _rec_inputs():
        import jax
        import jax.numpy as jnp
        _rk = jax.random.key(seed)
        x = -0.000125 + 0.9999 * jax.random.normal(jax.random.fold_in(_rk, 1), (16, 128, 256), jnp.float32)
        _lenS = 128 - jax.random.randint(jax.random.fold_in(_rk, 7), (16,), 0, max(1, 128 // 4) + 1, jnp.int32)
        _lenS2 = 128 - jax.random.randint(jax.random.fold_in(_rk, 8), (16,), 0, max(1, 128 // 4) + 1, jnp.int32)
        _ctx_2048P = jax.random.normal(jax.random.fold_in(_rk, 11), (16, 16, 256), jnp.float32)
        _ctx_2048c = jax.random.dirichlet(jax.random.fold_in(_rk, 511), 0.3 * jnp.ones((16,), jnp.float32), (16, 128))
        _ctx_2048t = jnp.einsum('bsk,bkd->bsd', _ctx_2048c, _ctx_2048P)
        _ctx_2048t = _ctx_2048t * jax.lax.rsqrt(jnp.mean(jnp.square(_ctx_2048t)) + 1e-12) * 0.953939
        ctx_2048 = -1.52775e-05 + 0.999936 * (_ctx_2048t + 0.3 * jax.random.normal(jax.random.fold_in(_rk, 611), (16, 128, 256), jnp.float32))
        _validS = jnp.arange(128)[None, :] < _lenS[:, None]
        _validS2 = jnp.arange(128)[None, :] < _lenS2[:, None]
        _causal = jnp.tril(jnp.ones((128, 128), dtype=bool))
        mask_BxSxS2_ff0 = jnp.where(jnp.ones((16, 128, 128), dtype=bool), 0.0, -1000000000.0).astype(jnp.float32)
        _g = jax.random.normal(jax.random.fold_in(_rk, 9001), (2, 2), jnp.float32)
        _g = jnp.sign(_g) * jnp.maximum(jnp.abs(_g), 1.0) + (_g == 0) * 1.0
        g_xattn = _g[0]
        g_ffn = _g[1]
        return (x, ctx_2048, mask_BxSxS2_ff0, g_xattn, g_ffn)
    x, ctx_2048, mask_BxSxS2_ff0, g_xattn, g_ffn = _rec_inputs()

    def _L0_xattn_setup():
        import jax, jax.numpy as jnp
        import numpy as np
        B, DIM1, DIM2, LATENT, T = (16, 128, 128, 64, 256)
        LN_EPS = 1e-05
        key = jax.random.key(seed)
        ks = jax.random.split(key, 8)

        def xavier(k, shape):
            fan_out, fan_in = shape
            std = float(np.sqrt(2.0 / (fan_in + fan_out)))
            return jax.random.normal(k, shape, dtype=jnp.float32) * std
        return {'input1': jax.random.normal(ks[0], (B, DIM1, T), dtype=jnp.float32), 'input2': jax.random.normal(ks[1], (B, DIM2, T), dtype=jnp.float32), 'theta_w': xavier(ks[2], (LATENT, DIM2)), 'theta_b': jnp.zeros((LATENT,), jnp.float32), 'phi_w': xavier(ks[3], (LATENT, DIM1)), 'phi_b': jnp.zeros((LATENT,), jnp.float32), 'g_w': xavier(ks[4], (LATENT, DIM1)), 'g_b': jnp.zeros((LATENT,), jnp.float32), 'ln_gamma': jnp.ones((LATENT, T), jnp.float32), 'ln_beta': jnp.zeros((LATENT, T), jnp.float32), 'out_w': xavier(ks[5], (DIM2, LATENT)), 'out_b': jnp.zeros((DIM2,), jnp.float32)}
    _L0_xattn_all = _L0_xattn_setup()
    _L0_xattn_in = {k: v for k, v in _L0_xattn_all.items() if k in ('theta_w', 'theta_b', 'phi_w', 'phi_b', 'g_w', 'g_b', 'ln_gamma', 'ln_beta', 'out_w', 'out_b')}
    del _L0_xattn_all

    def _L0_ffn_setup():
        import jax, jax.numpy as jnp
        import numpy as np
        TOPK = 2
        NORM_TOPK = True
        SCALE = 1.0
        EPS = 1e-09
        key = jax.random.key(seed)
        ks = jax.random.split(key, 9)
        h, i, E = (256, 128, 16)
        std = 0.02
        return {'x': jax.random.normal(ks[0], (1, 256, h), jnp.float32), 'Wr': jax.random.normal(ks[1], (E, h), jnp.float32) * std, 'bias': jnp.zeros((E,), jnp.float32), 'Wg': jax.random.normal(ks[2], (E, h, i), jnp.float32) * std, 'Wu': jax.random.normal(ks[3], (E, h, i), jnp.float32) * std, 'Wd': jax.random.normal(ks[4], (E, i, h), jnp.float32) * std, 'sWg': jax.random.normal(ks[5], (h, i), jnp.float32) * std, 'sWu': jax.random.normal(ks[6], (h, i), jnp.float32) * std, 'sWd': jax.random.normal(ks[7], (i, h), jnp.float32) * std}
    _L0_ffn_all = _L0_ffn_setup()
    _L0_ffn_in = {k: v for k, v in _L0_ffn_all.items() if k in ('Wr', 'bias', 'Wg', 'Wu', 'Wd', 'sWg', 'sWu', 'sWd')}
    del _L0_ffn_all

    def _L1_xattn_setup():
        import jax, jax.numpy as jnp
        import numpy as np
        B, Q_LEN, E = (8, 16, 256)
        CACHE_LEN = 512
        key = jax.random.key(seed)
        ks = jax.random.split(key, 9)
        s = 1.0 / np.sqrt(E)
        return {'x': jax.random.normal(ks[0], (B, Q_LEN, E), jnp.float32), 'attention_mask': jnp.zeros((B, Q_LEN, CACHE_LEN), jnp.float32), 'k_cache': jax.random.normal(ks[1], (B, CACHE_LEN, E), jnp.float32), 'v_cache': jax.random.normal(ks[2], (B, CACHE_LEN, E), jnp.float32), 'Wq': jax.random.normal(ks[3], (E, E), jnp.float32) * s, 'bq': jax.random.normal(ks[4], (E,), jnp.float32) * s, 'Wk': jax.random.normal(ks[5], (E, E), jnp.float32) * s, 'bk': jax.random.normal(ks[6], (E,), jnp.float32) * s, 'Wv': jax.random.normal(ks[7], (E, E), jnp.float32) * s, 'bv': jax.random.normal(ks[8], (E,), jnp.float32) * s}
    _L1_xattn_all = _L1_xattn_setup()
    _L1_xattn_in = {k: v for k, v in _L1_xattn_all.items() if k in ('Wq', 'bq', 'Wk', 'bk', 'Wv', 'bv')}
    del _L1_xattn_all

    def _L1_ffn_setup():
        import jax, jax.numpy as jnp
        import numpy as np
        B, S, H = (4, 128, 256)
        E, K, I, SI = (16, 4, 176, 704)

        def _silu_mul(gu, inter):
            return jax.nn.silu(gu[:, :inter]) * gu[:, inter:]
        key = jax.random.key(seed)
        ks = jax.random.split(key, 7)
        s = 0.02
        return {'hidden_states': jax.random.normal(ks[0], (B, S, H), jnp.float32), 'gate_w': jax.random.normal(ks[1], (E, H), jnp.float32) * s, 'expert_gate_up': jax.random.normal(ks[2], (E, 2 * I, H), jnp.float32) * s, 'expert_down': jax.random.normal(ks[3], (E, H, I), jnp.float32) * s, 'shared_gate_up': jax.random.normal(ks[4], (2 * SI, H), jnp.float32) * s, 'shared_down': jax.random.normal(ks[5], (H, SI), jnp.float32) * s, 'shared_gate_vec': jax.random.normal(ks[6], (1, H), jnp.float32) * s}
    _L1_ffn_all = _L1_ffn_setup()
    _L1_ffn_in = {k: v for k, v in _L1_ffn_all.items() if k in ('gate_w', 'expert_gate_up', 'expert_down', 'shared_gate_up', 'shared_down', 'shared_gate_vec')}
    del _L1_ffn_all
    return {'x': x, 'ctx_2048': ctx_2048, 'mask_BxSxS2_ff0': mask_BxSxS2_ff0, 'g_xattn': g_xattn, 'g_ffn': g_ffn, 'L0_xattn_theta_w': _L0_xattn_in['theta_w'], 'L0_xattn_theta_b': _L0_xattn_in['theta_b'], 'L0_xattn_phi_w': _L0_xattn_in['phi_w'], 'L0_xattn_phi_b': _L0_xattn_in['phi_b'], 'L0_xattn_g_w': _L0_xattn_in['g_w'], 'L0_xattn_g_b': _L0_xattn_in['g_b'], 'L0_xattn_ln_gamma': _L0_xattn_in['ln_gamma'], 'L0_xattn_ln_beta': _L0_xattn_in['ln_beta'], 'L0_xattn_out_w': _L0_xattn_in['out_w'], 'L0_xattn_out_b': _L0_xattn_in['out_b'], 'L0_ffn_Wr': _L0_ffn_in['Wr'], 'L0_ffn_bias': _L0_ffn_in['bias'], 'L0_ffn_Wg': _L0_ffn_in['Wg'], 'L0_ffn_Wu': _L0_ffn_in['Wu'], 'L0_ffn_Wd': _L0_ffn_in['Wd'], 'L0_ffn_sWg': _L0_ffn_in['sWg'], 'L0_ffn_sWu': _L0_ffn_in['sWu'], 'L0_ffn_sWd': _L0_ffn_in['sWd'], 'L1_xattn_Wq': _L1_xattn_in['Wq'], 'L1_xattn_bq': _L1_xattn_in['bq'], 'L1_xattn_Wk': _L1_xattn_in['Wk'], 'L1_xattn_bk': _L1_xattn_in['bk'], 'L1_xattn_Wv': _L1_xattn_in['Wv'], 'L1_xattn_bv': _L1_xattn_in['bv'], 'L1_ffn_gate_w': _L1_ffn_in['gate_w'], 'L1_ffn_expert_gate_up': _L1_ffn_in['expert_gate_up'], 'L1_ffn_expert_down': _L1_ffn_in['expert_down'], 'L1_ffn_shared_gate_up': _L1_ffn_in['shared_gate_up'], 'L1_ffn_shared_down': _L1_ffn_in['shared_down'], 'L1_ffn_shared_gate_vec': _L1_ffn_in['shared_gate_vec']}

def reference(x, ctx_2048, mask_BxSxS2_ff0, g_xattn, g_ffn, L0_xattn_theta_w, L0_xattn_theta_b, L0_xattn_phi_w, L0_xattn_phi_b, L0_xattn_g_w, L0_xattn_g_b, L0_xattn_ln_gamma, L0_xattn_ln_beta, L0_xattn_out_w, L0_xattn_out_b, L0_ffn_Wr, L0_ffn_bias, L0_ffn_Wg, L0_ffn_Wu, L0_ffn_Wd, L0_ffn_sWg, L0_ffn_sWu, L0_ffn_sWd, L1_xattn_Wq, L1_xattn_bq, L1_xattn_Wk, L1_xattn_bk, L1_xattn_Wv, L1_xattn_bv, L1_ffn_gate_w, L1_ffn_expert_gate_up, L1_ffn_expert_down, L1_ffn_shared_gate_up, L1_ffn_shared_down, L1_ffn_shared_gate_vec):
    import jax
    import jax.numpy as jnp

    def _L0_xattn_ref(input1, input2, theta_w, theta_b, phi_w, phi_b, g_w, g_b, ln_gamma, ln_beta, out_w, out_b):
        import jax, jax.numpy as jnp
        import numpy as np
        B, DIM1, DIM2, LATENT, T = (16, 128, 128, 64, 256)
        LN_EPS = 1e-05
        theta_x = jnp.einsum('ld,bdt->btl', theta_w, input2) + theta_b
        phi_x = jnp.einsum('ld,bdt->blt', phi_w, input1) + phi_b[:, None]
        scores = jnp.einsum('btl,bls->bts', theta_x, phi_x)
        p = jax.nn.softmax(scores, axis=-1)
        g_x = jnp.einsum('ld,bdt->btl', g_w, input1) + g_b
        t_x = jnp.einsum('bts,bsl->blt', p, g_x)
        mu = jnp.mean(t_x, axis=(1, 2), keepdims=True)
        var = jnp.var(t_x, axis=(1, 2), keepdims=True)
        h = (t_x - mu) * jax.lax.rsqrt(var + LN_EPS) * ln_gamma + ln_beta
        h = jax.nn.relu(h)
        w_t = jnp.einsum('ol,blt->bot', out_w, h) + out_b[None, :, None]
        return w_t + input2

    def _L0_ffn_ref(x, Wr, bias, Wg, Wu, Wd, sWg, sWu, sWd):
        import jax, jax.numpy as jnp
        import numpy as np
        TOPK = 2
        NORM_TOPK = True
        SCALE = 1.0
        EPS = 1e-09
        b, s, h = x.shape
        E = Wr.shape[0]
        xt = x.reshape(b * s, h)
        logits = xt @ Wr.T + bias
        probs = jax.nn.softmax(logits, axis=-1)
        topk_val, topk_idx = jax.lax.top_k(probs, TOPK)
        if NORM_TOPK:
            w = topk_val / (jnp.sum(topk_val, axis=-1, keepdims=True) + EPS)
        else:
            w = topk_val
        w = w * SCALE
        g = jnp.einsum('th,ehi->tei', xt, Wg)
        u = jnp.einsum('th,ehi->tei', xt, Wu)
        y = jnp.einsum('tei,eih->teh', jax.nn.silu(g) * u, Wd)
        oh = jax.nn.one_hot(topk_idx, E, dtype=x.dtype)
        routed = jnp.einsum('tke,tk,teh->th', oh, w, y)
        shared = jax.nn.silu(xt @ sWg) * (xt @ sWu) @ sWd
        return (routed + shared).reshape(b, s, h)

    def _L1_xattn_ref(x, attention_mask, k_cache, v_cache, Wq, bq, Wk, bk, Wv, bv):
        import jax, jax.numpy as jnp
        import numpy as np
        B, Q_LEN, E = (8, 16, 256)
        CACHE_LEN = 512
        Q = jnp.einsum('bqe,fe->bqf', x, Wq) + bq
        K_new = jnp.einsum('bqe,fe->bqf', x, Wk) + bk
        V_new = jnp.einsum('bqe,fe->bqf', x, Wv) + bv
        q_len = x.shape[1]
        end_step = attention_mask.shape[-1]
        past_kv_len = end_step - q_len
        k_cache = jax.lax.dynamic_update_slice(k_cache, K_new, (0, past_kv_len, 0))
        v_cache = jax.lax.dynamic_update_slice(v_cache, V_new, (0, past_kv_len, 0))
        K = k_cache[:, :end_step, :]
        V = v_cache[:, :end_step, :]
        scale = 1.0 / jnp.sqrt(jnp.asarray(Q.shape[-1], Q.dtype))
        scores = jnp.einsum('bqe,bke->bqk', Q, K) * scale + attention_mask
        attn = jax.nn.softmax(scores, axis=-1)
        return jnp.einsum('bqk,bke->bqe', attn, V)

    def _L1_ffn_ref(hidden_states, gate_w, expert_gate_up, expert_down, shared_gate_up, shared_down, shared_gate_vec):
        import jax, jax.numpy as jnp
        import numpy as np
        B, S, H = (4, 128, 256)
        E, K, I, SI = (16, 4, 176, 704)

        def _silu_mul(gu, inter):
            return jax.nn.silu(gu[:, :inter]) * gu[:, inter:]
        orig_shape = hidden_states.shape
        x = hidden_states.reshape(-1, H)
        router_logits = x @ gate_w.T
        routing_probs = jax.nn.softmax(router_logits.astype(jnp.float32), axis=-1)
        topk_w, topk_idx = jax.lax.top_k(routing_probs, K)
        topk_w = topk_w / topk_w.sum(axis=-1, keepdims=True)
        topk_w = topk_w.astype(x.dtype)
        combine = (jax.nn.one_hot(topk_idx, E, dtype=x.dtype) * topk_w[..., None]).sum(1)
        shared = _silu_mul(x @ shared_gate_up.T, SI) @ shared_down.T
        shared = shared * jax.nn.sigmoid(x @ shared_gate_vec.T)

        def step(acc, ew):
            w_gu, w_d, cw = ew
            h = _silu_mul(x @ w_gu.T, I)
            return (acc + h @ w_d.T * cw[:, None], None)
        acc0 = jnp.zeros_like(x)
        sparse, _ = jax.lax.scan(step, acc0, (expert_gate_up, expert_down, combine.T))
        return (shared + sparse).reshape(orig_shape)
    x = x + jnp.tanh(g_xattn[0]) * _L0_xattn_ref(_layernorm(x, axis=-1), ctx_2048, L0_xattn_theta_w, L0_xattn_theta_b, L0_xattn_phi_w, L0_xattn_phi_b, L0_xattn_g_w, L0_xattn_g_b, L0_xattn_ln_gamma, L0_xattn_ln_beta, L0_xattn_out_w, L0_xattn_out_b)
    x = x + jnp.tanh(g_ffn[0]) * _L0_ffn_ref(_layernorm(x, axis=-1), L0_ffn_Wr, L0_ffn_bias, L0_ffn_Wg, L0_ffn_Wu, L0_ffn_Wd, L0_ffn_sWg, L0_ffn_sWu, L0_ffn_sWd)
    x = x + jnp.tanh(g_xattn[1]) * _L1_xattn_ref(_layernorm(x, axis=-1), mask_BxSxS2_ff0, ctx_2048, ctx_2048, L1_xattn_Wq, L1_xattn_bq, L1_xattn_Wk, L1_xattn_bk, L1_xattn_Wv, L1_xattn_bv)
    x = x + jnp.tanh(g_ffn[1]) * _L1_ffn_ref(_layernorm(x, axis=-1), L1_ffn_gate_w, L1_ffn_expert_gate_up, L1_ffn_expert_down, L1_ffn_shared_gate_up, L1_ffn_shared_down, L1_ffn_shared_gate_vec)
    return x

_drawn_inputs = setup_inputs


def setup_inputs(seed=0):
    import zlib

    import numpy as np

    out = dict(_drawn_inputs(seed))
    spreads = {'g_ffn': (-1.0, 0.6),
     'L0_xattn_theta_b': (0.0, 0.1),
     'L0_xattn_phi_b': (0.0, 2.0),
     'L0_xattn_g_b': (0.0, 0.1),
     'L0_xattn_ln_gamma': (1.0, 0.2),
     'L0_xattn_ln_beta': (0.0, 0.1),
     'L0_xattn_out_b': (0.0, 0.8),
     'L0_ffn_bias': (0.0, 0.8)}
    factors = {'L0_ffn_Wr': 8.0,
     'L0_ffn_Wg': 8.0,
     'L0_ffn_Wu': 8.0,
     'L0_ffn_Wd': 8.0,
     'L0_ffn_sWg': 8.0,
     'L0_ffn_sWu': 8.0,
     'L0_ffn_sWd': 8.0,
     'L1_xattn_bq': 8.0,
     'L1_xattn_bk': 64.0,
     'L1_ffn_gate_w': 8.0,
     'L1_ffn_expert_gate_up': 8.0,
     'L1_ffn_expert_down': 8.0,
     'L1_ffn_shared_gate_up': 6.856,
     'L1_ffn_shared_down': 6.845,
     'L1_ffn_shared_gate_vec': 8.0,
     'L1_xattn_bv': 4.06}
    for name, (base, spread) in spreads.items():
        noise = np.random.default_rng([zlib.crc32(name.encode()), seed]).standard_normal(out[name].shape)
        drawn = base * np.exp(spread * noise) if base else spread * noise
        out[name] = jnp.asarray(drawn.astype(out[name].dtype))
    for name, factor in factors.items():
        out[name] = (out[name] * factor).astype(out[name].dtype)
    return out
```

```python
from contextlib import ExitStack

import concourse.bass as bass
from concourse import mybir

F32 = mybir.dt.float32
F32R = mybir.dt.float32r
BF16 = mybir.dt.bfloat16
ALU = mybir.AluOpType
ACT = mybir.ActivationFunctionType
AX_X = mybir.AxisListType.X

P = 128
NB, D = 16, 256
DC = D // P
LAT = 64
BLK = 512
NBLK = NB * P // BLK
PER = BLK // P
NE = 16
NCW = NE + 1
NL = NCW + 1
NSENT = 8
WGU, WD = 2 * DC * P, D
WT = WGU + WD
TILES = (17, 28)
TOPK = (2, 4)
TOPK_EPS = 1e-9
LN_EPS = 1e-5
SLOTS = 4


def gated_blocks(nc, x_in, ctx_in, mask_in, gates_in, ident_in, identb_in,
                 lat_w, lat_b, lat_out_w, lat_out_b, lat_norm,
                 qkv_w, qk_b, v_b, router_w, router_b, ffn_w, sel_in, out):
    with ExitStack() as ctx:
        def sb(name, shape, dt=F32):
            return ctx.enter_context(nc.sbuf_tensor(name, shape, dt))

        def sem(name):
            return ctx.enter_context(nc.semaphore(name))

        x = sb("x", [P, NB, D])
        xn = sb("xn", [P, NB, D])
        xT_hi = sb("xT_hi", [P, DC, NB * P], F32R)
        xT_lo = sb("xT_lo", [P, DC, NB * P], F32R)
        ctx_accT = sb("ctx_accT", [P, NB * D])
        ctx_sb = ctx_accT[:, :].rearrange("p (b d) -> p b d", b=NB)
        accT = ctx_accT[:, :].rearrange("p (c n) -> p c n", c=DC)
        mask = sb("mask", [P, NB, P])
        ident = sb("ident", [P, P])
        identb = sb("identb", [P, P], BF16)
        tg = sb("tg", [P, 4])
        mhalf = sb("mhalf", [P, NB])
        ones = sb("ones", [LAT, LAT])
        bn6 = sb("bn6", [P, NB, 6])
        mv = sb("mv", [P, NB, 2])
        ve = sb("ve", [P, NB])
        rstd = sb("rstd", [P, NB])
        lw = sb("lw", [P, 3, LAT])
        lb = sb("lb", [LAT, 3])
        low = sb("low", [LAT, P])
        lob = sb("lob", [P, 1])
        lnorm = sb("lnorm", [LAT, 2, D])
        shared_bufs = sb("shared_bufs", [P, 6400])
        at = [0]

        def part(n, rows=P):
            a = at[0]
            at[0] += n
            return shared_bufs[0:rows, a:a + n]

        thph = [part(2 * D, LAT).rearrange("p (a t) -> p a t", a=2) for _ in range(2)]
        g_sb = [part(2 * LAT) for _ in range(4)]
        p_sb = [part(2 * D).rearrange("p (c s) -> p c s", c=2) for _ in range(2)]
        pT_sb = [part(2 * D) for _ in range(2)]
        tx = [part(D, LAT) for _ in range(4)]
        hu = [part(D, LAT) for _ in range(2)]
        hv = [part(D, LAT) for _ in range(2)]
        hr = [part(D, LAT) for _ in range(2)]
        wt = part(D)
        assert at[0] <= 6400
        at[0] = 0
        QT = [part(DC * BLK).rearrange("p (c n) -> p c n", c=DC) for _ in range(2)]
        KT = [part(DC * BLK).rearrange("p (c n) -> p c n", c=DC) for _ in range(2)]
        V_sb = [part(D) for _ in range(2)]
        sm = [part(P) for _ in range(2)]
        pr = [part(P) for _ in range(2)]
        prT = [part(P) for _ in range(2)]
        ot = part(D)
        assert at[0] <= 6400
        nmx = sb("nmx", [P, 2, 2])
        rs = sb("rs", [P, 2, 2])
        rr = sb("rr", [P, 2, 2])
        tx6 = sb("tx6", [LAT, 2, 6])
        txmv = sb("txmv", [LAT, 2, 2])
        mu = sb("mu", [LAT, 4, 1])
        dmu = sb("dmu", [LAT, 2, 1])
        q2 = sb("q2", [LAT, 2, 1])
        hve = sb("hve", [LAT, 2, 1])
        hrstd = sb("hrstd", [LAT, 2, 1])
        qkv_raw = sb("qkv_raw", [P, 3 * DC * D])
        qkv_hi = sb("qkv_hi", [P, 3 * DC * D], F32R)
        qkv_lo = sb("qkv_lo", [P, 3 * DC * D], F32R)
        qkb = sb("qkb", [P, 2, DC])
        vb = sb("vb", [P, D])
        nmx1 = sb("nmx1", [P, 2, 1])
        rs1 = sb("rs1", [P, 4, 1])
        rr1 = sb("rr1", [P, 2, 1])
        rw_raw = sb("rw_raw", [P, 2, DC * NL])
        rw_hi = sb("rw_hi", [P, 2, DC * NL], F32R)
        rw_lo = sb("rw_lo", [P, 2, DC * NL], F32R)
        rb = sb("rb", [P, NE])
        z = sb("z", [P, NB, NCW])
        ez = sb("ez", [P, NB, NE])
        es = sb("es", [P, NB])
        rowst = sb("rowst", [P, NB])
        rowrc = sb("rowrc", [P, NB])
        probs = sb("probs", [P, NB, NE + NSENT])
        rest = sb("rest", [P, NB, NE + NSENT])
        top8 = sb("top8", [P, NB, 8])
        cw = sb("cw", [P, NB, NCW])
        cwr = sb("cwr", [P, NB, NCW])
        cw3 = sb("cw3", [P, NB, 3 * NCW], BF16)
        cwT = sb("cwT", [3 * NCW, NB * P], BF16)
        w_raw = sb("w_raw", [P, SLOTS, WT])
        w_hi = sb("w_hi", [P, SLOTS, WT], F32R)
        w_lo = sb("w_lo", [P, SLOTS, WT], F32R)
        sel = sb("sel", [3 * NCW, SLOTS, P], BF16)
        sg = sb("sg", [P, 2, BLK])
        gu = sb("gu", [P, BLK])
        hh = sb("hh", [P, 2, BLK])
        h_hi = sb("h_hi", [P, 2, BLK], F32R)
        h_lo = sb("h_lo", [P, 2, BLK], F32R)

        bank = [ctx.enter_context(nc.psum_tensor(f"bank{i}", [P, BLK], F32)) for i in range(6)]
        pair_bank = ctx.enter_context(nc.psum_tensor("pair_bank", [P, DC, BLK], F32))
        bank += [pair_bank[:, c, :] for c in range(DC)]

        x_in_ok = [sem(f"x_in_ok{g}") for g in range(NBLK)]
        small_ok, ctx_ok, later_ok, out_ok = sem("small_ok"), sem("ctx_ok"), sem("later_ok"), sem("out_ok")
        tanh_ok, const_ok, rw_hi_ok, rw_lo_ok = sem("tanh_ok"), sem("const_ok"), sem("rw_hi_ok"), sem("rw_lo_ok")
        qkv_hi_ok, qkv_lo_ok = sem("qkv_hi_ok"), sem("qkv_lo_ok")
        N_SMALL, N_LATER = 10, 6

        names = ("stats", "aggr", "var", "rstd", "xn", "xTp", "hi", "lo")
        norm = [dict(zip(names, (sem(f"norm{n}_{s}") for s in names))) for n in range(4)]
        names = ("logits", "exp", "cw", "cwT", "turned", "step", "sent")
        rout = [dict(zip(names, (sem(f"router{n}_{s}") for s in names))) for n in range(2)]
        names = ("w_hi", "w_lo", "c", "g", "u", "silu", "gu", "h", "h_hi", "h_lo", "down", "summed", "zero",
                 "turned", "x")
        ffn = [dict(zip(names, (sem(f"ffn{n}_{s}") for s in names))) for n in range(2)]
        raw_ok = [[sem(f"raw{n}_ok{s}") for s in range(SLOTS)] for n in range(2)]
        sel_ok = [[sem(f"sel{n}_ok{s}") for s in range(SLOTS)] for n in range(2)]
        names = ("thph", "g", "thph_sb", "g_sb", "sc", "max", "exp", "rec", "p", "pT", "pT_sb", "tx", "tx_sb",
                 "st", "ag", "m1", "mu", "d", "q", "m2", "var", "rstd", "u", "v", "h", "w", "c", "x")
        a0 = dict(zip(names, (sem(f"lat_{s}") for s in names)))
        names = ("proj", "proj_sb", "v", "v_sb", "sc", "sm", "max", "exp", "rec", "pT", "pT_sb", "o", "t", "x")
        a1 = dict(zip(names, (sem(f"att_{s}") for s in names)))

        block = ctx.enter_context(nc.Block())

        def pairs_of(layer):
            n = TILES[layer] // SLOTS
            assert TILES[layer] - SLOTS * n <= 1
            return (n, TILES[layer] - SLOTS * n)

        def pair_done(round_, slot):
            return (round_ * 2 + slot // 2 - 1) * 2 * NBLK

        @block.sync
        def _(sp):
            for g in range(NBLK):
                sp.dma_start(x[:, PER * g:PER * g + PER, :],
                             x_in[PER * g:PER * g + PER].rearrange("b p d -> p b d")).then_inc(x_in_ok[g], 16)
            small = [(gates_in, tg), (ident_in, ident), (identb_in, identb), (lat_w, lw), (lat_b, lb),
                     (lat_out_w, low), (lat_out_b, lob), (lat_norm, lnorm), (router_w, rw_raw), (router_b, rb)]
            assert len(small) == N_SMALL
            for src, dst in small:
                sp.dma_start(dst[:], src).then_inc(small_ok, 16)
            sp.dma_start(ctx_sb, ctx_in.rearrange("b p d -> p b d")).then_inc(ctx_ok, 16)
            later = [(qkv_w, qkv_raw[:]), (qk_b, qkb[:]), (v_b, vb[:])]
            for src, dst in later:
                sp.dma_start(dst, src).then_inc(later_ok, 16)
            sp.dma_start(mask[:], mask_in.rearrange("b p k -> p b k")).then_inc(later_ok, 16)

            def load_tile(layer, t, slot, round_):
                f = ffn[layer]
                again = not (isinstance(t, int) and t < SLOTS)
                if again:
                    sp.wait_ge(f["w_lo"], t - SLOTS + 1)
                elif layer == 1:
                    sp.wait_ge(ffn[0]["w_lo"], TILES[0])
                sp.dma_start(w_raw[:, slot, :], ffn_w[layer][t]).then_inc(raw_ok[layer][slot], 16)
                if again:
                    sp.wait_ge(f["down"], pair_done(round_, slot))
                elif layer == 1:
                    sp.wait_ge(ffn[0]["down"], TILES[0] * NBLK)
                sp.dma_start(sel[:, slot, :], sel_in[layer][t]).then_inc(sel_ok[layer][slot], 16)

            for layer in range(2):
                n, left = pairs_of(layer)
                for s in range(SLOTS):
                    load_tile(layer, s, s, 0)
                with sp.Fori(1, n) as i:
                    for s in range(SLOTS):
                        load_tile(layer, i * SLOTS + s, s, i)
                for s in range(left):
                    load_tile(layer, n * SLOTS + s, s, n)
            for k in range(NB):
                sp.wait_ge(ffn[1]["x"], k + 1)
                sp.dma_start(out[k], x[:, k, :]).then_inc(out_ok, 16)
            sp.wait_ge(out_ok, 16 * NB)

        @block.gpsimd
        def _(pool):
            pool.memset(mhalf[:], -0.5).then_inc(const_ok, 1)
            pool.memset(ones[:], 1.0 / LAT).then_inc(const_ok, 1)
            pool.memset(probs[:], -1.0).then_inc(const_ok, 1)
            pool.wait_ge(const_ok, 3)

            def row_rstd(n):
                s = norm[n]
                for g in range(NBLK):
                    b = slice(PER * g, PER * g + PER)
                    pool.wait_ge(s["var"], g + 1)
                    pool.tensor_tensor(rstd[:, b], ve[:, b], mhalf[:, b], ALU.pow).then_inc(s["rstd"], 1)

            row_rstd(0)
            for b in range(NB):
                pool.wait_ge(a0["var"], b + 1)
                pool.tensor_tensor(hrstd[:, b % 2, :], hve[:, b % 2, :], mhalf[0:LAT, 0:1], ALU.pow)\
                    .then_inc(a0["rstd"], 1)
            pool.wait_ge(a0["x"], NB)
            pool.memset(ctx_accT[:], 0.0).then_inc(ffn[0]["zero"], 1)
            row_rstd(1)
            row_rstd(2)
            pool.wait_ge(ffn[0]["x"], NB)
            pool.memset(ctx_accT[:], 0.0).then_inc(ffn[1]["zero"], 1)
            row_rstd(3)

        @block.scalar
        def _(act):
            act.wait_ge(small_ok, 16 * N_SMALL)
            act.activation(tg[:], tg[:], ACT.Tanh).then_inc(tanh_ok, 1)
            act.activation(rw_hi[:], rw_raw[:], ACT.Copy).then_inc(rw_hi_ok, 1)

            def split_xT(n):
                s = norm[n]
                for k in range(NB):
                    act.wait_ge(s["xTp"], k + 1)
                    act.activation(xT_hi[:, :, k * P:k * P + P],
                                   bank[k % 2][:, 0:D].rearrange("p (c n) -> p c n", c=DC),
                                   ACT.Copy).then_inc(s["hi"], 1)

            def thph_out(b):
                act.wait_ge(a0["thph"], b + 1)
                if b >= 2:
                    act.wait_ge(a0["sc"], b - 1)
                act.activation(thph[b % 2][:, 0, :], bank[0][0:LAT, 0:D], ACT.Identity, bias=lb[:, 0:1])\
                    .then_inc(a0["thph_sb"], 1)
                act.activation(thph[b % 2][:, 1, :], bank[0][0:LAT, D:2 * D], ACT.Identity, bias=lb[:, 1:2])\
                    .then_inc(a0["thph_sb"], 1)

            def exps(b):
                act.wait_ge(a0["max"], b + 1)
                if b >= 2:
                    act.wait_ge(a0["pT"], b - 1)
                for c in range(2):
                    act.activation(p_sb[b % 2][:, c, :], bank[2][:, c * D:c * D + D], ACT.Exp,
                                   bias=nmx[:, b % 2, c:c + 1], accum_out=rs[:, b % 2, c:c + 1])\
                        .then_inc(a0["exp"], 1)

            def pT_out(b):
                act.wait_ge(a0["pT"], b + 1)
                if b >= 2:
                    act.wait_ge(a0["tx"], b - 1)
                act.activation(pT_sb[b % 2], bank[3][:, :], ACT.Copy).then_inc(a0["pT_sb"], 1)

            def tx_out(b):
                act.wait_ge(a0["tx"], b + 1)
                if b >= 4:
                    act.wait_ge(a0["u"], b - 3)
                act.activation(tx[b % 4], bank[4][0:LAT, 0:D], ACT.Identity, bias=lb[:, 2:3])\
                    .then_inc(a0["tx_sb"], 1)

            def relu(b):
                act.wait_ge(a0["v"], b + 1)
                if b >= 2:
                    act.wait_ge(a0["w"], b - 1)
                act.activation(hr[b % 2], hv[b % 2], ACT.Relu).then_inc(a0["h"], 1)

            for i in range(NB + 6):
                if i < NB:
                    thph_out(i)
                if 0 <= i - 1 < NB:
                    exps(i - 1)
                if 0 <= i - 2 < NB:
                    pT_out(i - 2)
                if 0 <= i - 3 < NB:
                    tx_out(i - 3)
                if 0 <= i - 5 < NB:
                    relu(i - 5)
            act.wait_ge(later_ok, 16 * 4)
            act.activation(qkv_hi[:], qkv_raw[:], ACT.Copy).then_inc(qkv_hi_ok, 1)

            def router(layer):
                s = rout[layer]
                act.wait_ge(s["step"], 3)
                act.activation(ez[:], z[:, :, 0:NE], ACT.Exp).then_inc(s["exp"], 1)
                if layer == 1:
                    act.activation(es[:], z[:, :, NE], ACT.Exp, scale=-1.0).then_inc(s["exp"], 1)
                for j in range(2):
                    act.wait_ge(s["cwT"], 8 * j + 8)
                    act.activation(cwT[:, 8 * P * j:8 * P * j + 8 * P],
                                   bank[3 + j][0:3 * NCW, :].bitcast(BF16), ACT.Copy).then_inc(s["turned"], 1)

            def split_tile(layer, t, slot, round_):
                f = ffn[layer]
                act.wait_ge(raw_ok[layer][slot], 16 * (round_ + 1))
                if not (isinstance(t, int) and t < SLOTS):
                    act.wait_ge(f["down"], pair_done(round_, slot))
                elif layer == 1:
                    act.wait_ge(ffn[0]["down"], TILES[0] * NBLK)
                act.activation(w_hi[:, slot, :], w_raw[:, slot, :], ACT.Copy).then_inc(f["w_hi"], 1)

            def hidden(layer, n, par, first):
                f = ffn[layer]
                act.wait_ge(f["g"], n + 1)
                if not first:
                    act.wait_ge(f["gu"], n - 1)
                act.activation(sg[:, par, :], bank[par][:, :], ACT.Silu).then_inc(f["silu"], 1)
                act.wait_ge(f["h"], n + 1)
                if not first:
                    act.wait_ge(f["down"], n - 1)
                act.activation(h_hi[:, par, :], hh[:, par, :], ACT.Copy).then_inc(f["h_hi"], 1)

            def experts(layer):
                n_loop, left = pairs_of(layer)
                split_tile(layer, 0, 0, 0)
                split_tile(layer, 1, 1, 0)

                def body(i, last):
                    for q in range(2):
                        for m in range(2 * NBLK):
                            k = q * 2 * NBLK + m
                            hidden(layer, i * 4 * NBLK + k, m % 2, first=isinstance(i, int) and i == 0 and k < 2)
                            if m in (3, 5):
                                slot = (2 * q + 2 + (m == 5)) % SLOTS
                                if q == 0:
                                    split_tile(layer, i * SLOTS + slot, slot, i)
                                elif not last or slot < left:
                                    split_tile(layer, i * SLOTS + SLOTS + slot, slot, i + 1)

                body(0, False)
                with act.Fori(1, n_loop - 1) as i:
                    body(i, False)
                body(n_loop - 1, True)
                for m in range(left * NBLK):
                    hidden(layer, n_loop * 4 * NBLK + m, m % 2, False)

            split_xT(1)
            router(0)
            experts(0)
            split_xT(2)

            def proj_out(B):
                for j in range(2 * DC):
                    n = 2 * DC * B + j
                    act.wait_ge(a1["proj"], n + 1)
                    if B >= 2:
                        act.wait_ge(a1["sc"], PER * (B - 1))
                    dst = (QT, KT)[j // DC][B % 2]
                    act.activation(dst[:, j % DC, :], bank[j % 2][:, :], ACT.Identity,
                                   bias=qkb[:, j // DC, j % DC:j % DC + 1]).then_inc(a1["proj_sb"], 1)

            def v_out(b):
                act.wait_ge(a1["v"], b + 1)
                if b >= 2:
                    act.wait_ge(a1["o"], b - 1)
                act.activation(V_sb[b % 2], bank[2][:, 0:D], ACT.Copy).then_inc(a1["v_sb"], 1)

            def exp1(b):
                act.wait_ge(a1["max"], b + 1)
                if b >= 2:
                    act.wait_ge(a1["pT"], b - 1)
                if b >= 4:
                    act.wait_ge(a1["rec"], b - 3)
                act.activation(pr[b % 2], sm[b % 2], ACT.Exp, bias=nmx1[:, b % 2, :],
                               accum_out=rs1[:, b % 4, :]).then_inc(a1["exp"], 1)

            def prT_out(b):
                act.wait_ge(a1["pT"], b + 1)
                if b >= 2:
                    act.wait_ge(a1["o"], b - 1)
                act.activation(prT[b % 2], bank[4][:, 0:P], ACT.Copy).then_inc(a1["pT_sb"], 1)

            proj_out(0)
            for i in range(NB + 2):
                if i < NB:
                    v_out(i)
                if i % PER == 2 and i // PER + 1 < NBLK:
                    proj_out(i // PER + 1)
                if i < NB:
                    exp1(i)
                if 0 <= i - 1 < NB:
                    prT_out(i - 1)

            split_xT(3)
            router(1)
            experts(1)

        @block.vector
        def _(dve):
            dve.wait_ge(small_ok, 16 * N_SMALL)
            dve.wait_ge(rw_hi_ok, 1)
            dve.tensor_tensor(rw_lo[:], rw_raw[:], rw_hi[:].bitcast(F32), ALU.subtract).then_inc(rw_lo_ok, 1)
            dve.wait_ge(tanh_ok, 1)

            def row_norm(n, before, x_sem, transposed):
                s = norm[n]

                def low_part(k):
                    dve.wait_ge(s["hi"], k + 1)
                    dst = slice(k * P, k * P + P)
                    dve.tensor_tensor(xT_lo[:, :, dst], bank[k % 2][:, 0:D].rearrange("p (c n) -> p c n", c=DC),
                                      xT_hi[:, :, dst].bitcast(F32), ALU.subtract).then_inc(s["lo"], 1)

                for g in range(NBLK + 1):
                    if g < NBLK:
                        before(g)
                        if x_sem is not None:
                            dve.wait_ge(x_sem, PER * g + PER)
                        for k in range(PER * g, PER * g + PER):
                            dve.bn_stats(bn6[:, k, :], x[:, k, :]).then_inc(s["stats"], 1)
                        for k in range(PER * g, PER * g + PER):
                            dve.wait_ge(s["stats"], k + 1)
                            dve.bn_aggr(mv[:, k, :], bn6[:, k, :]).then_inc(s["aggr"], 1)
                        dve.wait_ge(s["aggr"], PER * g + PER)
                        b = slice(PER * g, PER * g + PER)
                        dve.tensor_scalar(ve[:, b], mv[:, b, 1], LN_EPS, None, ALU.add).then_inc(s["var"], 1)
                    if g >= 1:
                        dve.wait_ge(s["rstd"], g)
                        for k in range(PER * g - PER, PER * g):
                            dve.tensor_scalar(xn[:, k, :], x[:, k, :], mv[:, k, 0:1], rstd[:, k:k + 1],
                                              ALU.subtract, ALU.mult).then_inc(s["xn"], 1)
                            if transposed and k >= 2:
                                low_part(k - 2)
                if transposed:
                    low_part(NB - 2)
                    low_part(NB - 1)

            row_norm(0, lambda g: dve.wait_ge(x_in_ok[g], 16), None, False)

            def g_out(b):
                dve.wait_ge(a0["g"], b + 1)
                if b >= 4:
                    dve.wait_ge(a0["tx"], b - 3)
                dve.tensor_copy(g_sb[b % 4], bank[1][:, 0:2 * LAT]).then_inc(a0["g_sb"], 1)

            def maxes(b):
                dve.wait_ge(a0["sc"], b + 1)
                if b >= 2:
                    dve.wait_ge(a0["exp"], 2 * (b - 1))
                dve.tensor_reduce(nmx[:, b % 2, :], bank[2][:, :].rearrange("p (c s) -> p c s", c=2), AX_X,
                                  ALU.max, negate=True).then_inc(a0["max"], 1)

            def normalise_p(b):
                dve.wait_ge(a0["exp"], 2 * (b + 1))
                dve.reciprocal(rr[:, b % 2, :], rs[:, b % 2, :]).then_inc(a0["rec"], 1)
                dve.wait_ge(a0["rec"], b + 1)
                for c in range(2):
                    dve.tensor_scalar(p_sb[b % 2][:, c, :], p_sb[b % 2][:, c, :], rr[:, b % 2, c:c + 1], None,
                                      ALU.mult).then_inc(a0["p"], 1)

            def tx_stats(b):
                dve.wait_ge(a0["tx_sb"], b + 1)
                dve.bn_stats(tx6[:, b % 2, :], tx[b % 4]).then_inc(a0["st"], 1)
                dve.wait_ge(a0["st"], b + 1)
                if b >= 2:
                    dve.wait_ge(a0["m1"], b - 1)
                dve.bn_aggr(txmv[:, b % 2, :], tx6[:, b % 2, :]).then_inc(a0["ag"], 1)

            def tx_mean(b):
                dve.wait_ge(a0["m1"], b + 1)
                dve.tensor_copy(mu[:, b % 4, :], bank[5][0:LAT, 0:1]).then_inc(a0["mu"], 1)
                dve.wait_ge(a0["mu"], b + 1)
                dve.tensor_tensor(dmu[:, b % 2, :], txmv[:, b % 2, 0:1], mu[:, b % 4, :], ALU.subtract)\
                    .then_inc(a0["d"], 1)
                dve.wait_ge(a0["d"], b + 1)
                if b >= 2:
                    dve.wait_ge(a0["m2"], b - 1)
                dve.scalar_tensor_tensor(q2[:, b % 2, :], dmu[:, b % 2, :], dmu[:, b % 2, :],
                                         txmv[:, b % 2, 1:2], ALU.mult, ALU.add).then_inc(a0["q"], 1)

            def tx_var(b):
                dve.wait_ge(a0["m2"], b + 1)
                if b >= 2:
                    dve.wait_ge(a0["rstd"], b - 1)
                dve.tensor_scalar(hve[:, b % 2, :], bank[6][0:LAT, 0:1], LN_EPS, None, ALU.add)\
                    .then_inc(a0["var"], 1)
                dve.scalar_tensor_tensor(hu[b % 2], tx[b % 4], mu[:, b % 4, :], lnorm[:, 0, :],
                                         ALU.subtract, ALU.mult).then_inc(a0["u"], 1)

            def tx_scaled(b):
                dve.wait_ge(a0["rstd"], b + 1)
                dve.wait_ge(a0["u"], b + 1)
                if b >= 2:
                    dve.wait_ge(a0["h"], b - 1)
                dve.scalar_tensor_tensor(hv[b % 2], hu[b % 2], hrstd[:, b % 2, :], lnorm[:, 1, :],
                                         ALU.mult, ALU.add).then_inc(a0["v"], 1)

            def lat_add(b):
                dve.wait_ge(a0["w"], b + 1)
                dve.scalar_tensor_tensor(wt, bank[7][:, 0:D], lob[:, 0:1], ctx_sb[:, b, :],
                                         ALU.add, ALU.add).then_inc(a0["c"], 1)
                dve.wait_ge(a0["c"], b + 1)
                dve.scalar_tensor_tensor(x[:, b, :], wt, tg[:, 0:1], x[:, b, :],
                                         ALU.mult, ALU.add).then_inc(a0["x"], 1)

            dve.wait_ge(ctx_ok, 16)
            for i in range(NB + 7):
                if 0 <= i - 1 < NB:
                    maxes(i - 1)
                if i < NB:
                    g_out(i)
                if 0 <= i - 6 < NB:
                    lat_add(i - 6)
                if 0 <= i - 4 < NB:
                    tx_mean(i - 4)
                if 0 <= i - 1 < NB:
                    normalise_p(i - 1)
                if 0 <= i - 5 < NB:
                    tx_var(i - 5)
                if 0 <= i - 3 < NB:
                    tx_stats(i - 3)
                if 0 <= i - 5 < NB:
                    tx_scaled(i - 5)

            def router(layer):
                s = rout[layer]
                done = [0]

                def step(ins):
                    done[0] += 1
                    ins.then_inc(s["step"], 1)
                    dve.wait_ge(s["step"], done[0])

                def wide(v, n=NE):
                    return v.unsqueeze(2).to_broadcast([P, NB, n])

                dve.wait_ge(s["logits"], 1)
                lg = bank[2][:, 0:NB * NL].rearrange("p (b e) -> p b e", b=NB)
                if layer == 0:
                    step(dve.tensor_tensor(z[:, :, 0:NE], lg[:, :, 0:NE],
                                           rb[:].unsqueeze(1).to_broadcast([P, NB, NE]), ALU.add))
                else:
                    step(dve.tensor_copy(z[:], lg[:, :, 0:NCW]))
                step(dve.tensor_reduce(rowst[:], z[:, :, 0:NE], AX_X, ALU.max))
                step(dve.tensor_tensor(z[:, :, 0:NE], z[:, :, 0:NE], wide(rowst[:]), ALU.subtract))
                dve.wait_ge(s["exp"], 1 + layer)
                step(dve.tensor_reduce(rowst[:], ez[:], AX_X, ALU.add))
                step(dve.reciprocal(rowrc[:], rowst[:]))
                step(dve.tensor_tensor(probs[:, :, 0:NE], ez[:], wide(rowrc[:]), ALU.mult))
                for k in range(NB):
                    last = dve.max(top8[:, k, :], probs[:, k, 0:NE])
                step(last)
                step(dve.memset(top8[:, :, TOPK[layer]:8], -1.0))
                for k in range(NB):
                    last = dve.match_replace(rest[:, k, :], top8[:, k, :], probs[:, k, :], 0.0)
                step(last)
                step(dve.tensor_tensor(rest[:, :, 0:NE], probs[:, :, 0:NE], rest[:, :, 0:NE], ALU.subtract))
                step(dve.tensor_reduce(rowst[:], rest[:, :, 0:NE], AX_X, ALU.add))
                if layer == 0:
                    step(dve.tensor_scalar(rowst[:], rowst[:], TOPK_EPS, None, ALU.add))
                step(dve.reciprocal(rowrc[:], rowst[:]))
                step(dve.tensor_tensor(cw[:, :, 0:NE], rest[:, :, 0:NE], wide(rowrc[:]), ALU.mult))
                if layer == 0:
                    step(dve.memset(cw[:, :, NE:NCW], 1.0))
                else:
                    step(dve.tensor_scalar(es[:], es[:], 1.0, None, ALU.add))
                    step(dve.reciprocal(cw[:, :, NE], es[:]))
                step(dve.tensor_copy(cw3[:, :, 0:NCW], cw[:]))
                step(dve.tensor_tensor(cwr[:], cw[:], cw3[:, :, 0:NCW], ALU.subtract))
                step(dve.tensor_copy(cw3[:, :, NCW:2 * NCW], cwr[:]))
                step(dve.tensor_tensor(cwr[:], cwr[:], cw3[:, :, NCW:2 * NCW], ALU.subtract))
                dve.tensor_copy(cw3[:, :, 2 * NCW:3 * NCW], cwr[:]).then_inc(s["cw"], 1)

            def split_tile(layer, t):
                f = ffn[layer]
                slot = t[1]
                dve.wait_ge(f["w_hi"], t[0] + 1)
                dve.tensor_tensor(w_lo[:, slot, :], w_raw[:, slot, :], w_hi[:, slot, :].bitcast(F32),
                                  ALU.subtract).then_inc(f["w_lo"], 1)

            def add_sum(layer, downs, blk):
                f = ffn[layer]
                dve.wait_ge(f["down"], downs)
                dst = accT[:, :, blk * BLK:blk * BLK + BLK]
                dve.tensor_tensor(dst, pair_bank[:], dst, ALU.add).then_inc(f["summed"], 1)

            def hidden(layer, n, par, first, between):
                f = ffn[layer]
                dve.wait_ge(f["silu"], n + 1)
                dve.wait_ge(f["u"], n + 1)
                dve.wait_ge(f["h"], n)
                dve.tensor_tensor(gu[:], sg[:, par, :], bank[2 + par][:, :], ALU.mult).then_inc(f["gu"], 1)
                dve.wait_ge(f["gu"], n + 1)
                dve.wait_ge(f["c"], n + 1)
                if not first:
                    dve.wait_ge(f["h_lo"], n - 1)
                dve.tensor_tensor(hh[:, par, :], gu[:], bank[4 + par][:, :], ALU.mult).then_inc(f["h"], 1)
                between()
                dve.wait_ge(f["h_hi"], n + 1)
                dve.tensor_tensor(h_lo[:, par, :], hh[:, par, :], h_hi[:, par, :].bitcast(F32),
                                  ALU.subtract).then_inc(f["h_lo"], 1)

            def experts(layer):
                n_loop, left = pairs_of(layer)
                split_tile(layer, (0, 0))
                split_tile(layer, (1, 1))
                dve.wait_ge(ffn[layer]["zero"], 1)

                def body(i, first, last):
                    for q in range(2):
                        for m in range(2 * NBLK):
                            k = q * 2 * NBLK + m

                            def between():
                                if m % 2 == 0 and not (first and k == 0):
                                    add_sum(layer, i * 4 * NBLK + k, (m // 2 - 1) % NBLK)
                                if m in (3, 5):
                                    slot = (2 * q + 2 + (m == 5)) % SLOTS
                                    if q == 0:
                                        split_tile(layer, (i * SLOTS + slot, slot))
                                    elif not last or slot < left:
                                        split_tile(layer, (i * SLOTS + SLOTS + slot, slot))

                            hidden(layer, i * 4 * NBLK + k, m % 2, first and k < 2, between)

                body(0, True, False)
                with dve.Fori(1, n_loop - 1) as i:
                    body(i, False, False)
                body(n_loop - 1, False, True)
                steps = n_loop * 4 * NBLK
                for m in range(left * NBLK):
                    hidden(layer, n_loop * 4 * NBLK + m, m % 2, False,
                           lambda: add_sum(layer, steps + m, (m - 1) % NBLK))
                add_sum(layer, steps + left * NBLK, NBLK - 1)

            def finish(layer, g):
                f = ffn[layer]
                for k in range(PER * g, PER * g + PER):
                    dve.wait_ge(f["turned"], k + 1)
                    dve.scalar_tensor_tensor(x[:, k, :], bank[2 + k % 2][:, 0:D], tg[:, 2 + layer:3 + layer],
                                             x[:, k, :], ALU.mult, ALU.add).then_inc(f["x"], 1)

            row_norm(1, lambda g: None, a0["x"], True)
            dve.wait_ge(qkv_hi_ok, 1)
            dve.tensor_tensor(qkv_lo[:], qkv_raw[:], qkv_hi[:].bitcast(F32), ALU.subtract).then_inc(qkv_lo_ok, 1)
            dve.wait_ge(const_ok, 3)
            router(0)
            experts(0)
            row_norm(2, lambda g: finish(0, g), ffn[0]["x"], True)

            def masked(b):
                dve.wait_ge(a1["sc"], b + 1)
                if b >= 2:
                    dve.wait_ge(a1["exp"], b - 1)
                dve.scalar_tensor_tensor(sm[b % 2], bank[3][:, 0:P], float(D) ** -0.5, mask[:, b, :],
                                         ALU.mult, ALU.add).then_inc(a1["sm"], 1)
                dve.wait_ge(a1["sm"], b + 1)
                dve.tensor_reduce(nmx1[:, b % 2, :], sm[b % 2], AX_X, ALU.max, negate=True).then_inc(a1["max"], 1)

            def att_add(b):
                dve.wait_ge(a1["exp"], b + 1)
                dve.reciprocal(rr1[:, b % 2, :], rs1[:, b % 4, :]).then_inc(a1["rec"], 1)
                dve.wait_ge(a1["rec"], b + 1)
                dve.wait_ge(a1["o"], b + 1)
                dve.scalar_tensor_tensor(ot, bank[5][:, 0:D], rr1[:, b % 2, :], vb[:], ALU.mult, ALU.add)\
                    .then_inc(a1["t"], 1)
                dve.wait_ge(a1["t"], b + 1)
                dve.scalar_tensor_tensor(x[:, b, :], ot, tg[:, 1:2], x[:, b, :], ALU.mult, ALU.add)\
                    .then_inc(a1["x"], 1)

            dve.wait_ge(later_ok, 16 * 4)
            for i in range(NB + 2):
                if i < NB:
                    masked(i)
                if 0 <= i - 2 < NB:
                    att_add(i - 2)

            row_norm(3, lambda g: None, a1["x"], True)
            router(1)
            experts(1)
            for g in range(NBLK):
                finish(1, g)

        @block.tensor
        def _(pe):
            def mm3(dst, w, xv, start=True, stop=True):
                pe.matmul(dst, w[0], xv[0], start=start, stop=False)
                pe.matmul(dst, w[0], xv[1], start=False, stop=False)
                return pe.matmul(dst, w[1], xv[0], start=False, stop=stop)

            def mm3c(dst, ws, xs):
                for c in range(len(ws)):
                    last = mm3(dst, ws[c], xs[c], start=c == 0, stop=c == len(ws) - 1)
                return last

            def turn_rows(n, k):
                s = norm[n]
                pe.wait_ge(s["xn"], k + 1)
                if k >= 2:
                    pe.wait_ge(s["lo"], k - 1)
                for c in range(DC):
                    last = pe.transpose(bank[k % 2][:, c * P:c * P + P], xn[:, k, c * P:c * P + P], ident[:])
                last.then_inc(s["xTp"], 1)

            def xT(c, a, b):
                return (xT_hi[:, c, a:b], xT_lo[:, c, a:b])

            def latents(b):
                pe.wait_ge(norm[0]["xn"], b + 1)
                if b >= 1:
                    pe.wait_ge(a0["thph_sb"], 2 * b)
                pe.matmul(bank[0][0:LAT, 0:D], lw[:, 0, :], ctx_sb[:, b, :], start=True, stop=True)
                pe.matmul(bank[0][0:LAT, D:2 * D], lw[:, 1, :], xn[:, b, :], start=True, stop=True)\
                    .then_inc(a0["thph"], 1)
                if b >= 1:
                    pe.wait_ge(a0["g_sb"], b)
                for c in range(2):
                    last = pe.matmul(bank[1][:, c * LAT:c * LAT + LAT], xn[:, b, c * P:c * P + P], lw[:, 2, :],
                                     start=True, stop=True)
                last.then_inc(a0["g"], 1)

            def scores(b):
                pe.wait_ge(a0["thph_sb"], 2 * (b + 1))
                if b >= 1:
                    pe.wait_ge(a0["exp"], 2 * b)
                for c in range(2):
                    last = pe.matmul(bank[2][:, c * D:c * D + D], thph[b % 2][:, 0, c * P:c * P + P],
                                     thph[b % 2][:, 1, :], start=True, stop=True)
                last.then_inc(a0["sc"], 1)

            def turn_p(b):
                pe.wait_ge(a0["p"], 2 * (b + 1))
                if b >= 1:
                    pe.wait_ge(a0["pT_sb"], b)
                for j in range(2):
                    for c in range(2):
                        last = pe.transpose(bank[3][:, j * D + c * P:j * D + c * P + P],
                                            p_sb[b % 2][:, c, j * P:j * P + P], ident[:])
                last.then_inc(a0["pT"], 1)

            def weigh(b):
                pe.wait_ge(a0["pT_sb"], b + 1)
                pe.wait_ge(a0["g_sb"], b + 1)
                if b >= 1:
                    pe.wait_ge(a0["tx_sb"], b)
                for j in range(2):
                    last = pe.matmul(bank[4][0:LAT, 0:D], g_sb[b % 4][:, j * LAT:j * LAT + LAT],
                                     pT_sb[b % 2][:, j * D:j * D + D], start=j == 0, stop=j == 1)
                last.then_inc(a0["tx"], 1)

            def mean_rows(b):
                pe.wait_ge(a0["ag"], b + 1)
                if b >= 1:
                    pe.wait_ge(a0["mu"], b)
                pe.matmul(bank[5][0:LAT, 0:1], ones[:], txmv[:, b % 2, 0:1], start=True, stop=True)\
                    .then_inc(a0["m1"], 1)

            def var_rows(b):
                pe.wait_ge(a0["q"], b + 1)
                if b >= 1:
                    pe.wait_ge(a0["var"], b)
                pe.matmul(bank[6][0:LAT, 0:1], ones[:], q2[:, b % 2, :], start=True, stop=True)\
                    .then_inc(a0["m2"], 1)

            def lat_out(b):
                pe.wait_ge(a0["h"], b + 1)
                if b >= 1:
                    pe.wait_ge(a0["c"], b)
                pe.matmul(bank[7][:, 0:D], low[:], hr[b % 2], start=True, stop=True).then_inc(a0["w"], 1)

            pe.wait_ge(small_ok, 16 * N_SMALL)
            pe.wait_ge(ctx_ok, 16)
            pe.wait_ge(const_ok, 3)
            for i in range(NB + 6):
                if i < NB:
                    latents(i)
                if 0 <= i - 6 < NB:
                    lat_out(i - 6)
                if 0 <= i - 4 < NB:
                    mean_rows(i - 4)
                if 0 <= i - 1 < NB:
                    scores(i - 1)
                if 0 <= i - 2 < NB:
                    turn_p(i - 2)
                if 0 <= i - 5 < NB:
                    var_rows(i - 5)
                if 0 <= i - 3 < NB:
                    weigh(i - 3)

            def router(layer):
                s = rout[layer]
                pe.wait_ge(rw_lo_ok, 1)
                for k in range(NB):
                    pe.wait_ge(norm[1 + 2 * layer]["lo"], k + 1)
                    last = mm3c(bank[2][:, k * NL:k * NL + NL], [xT(c, k * P, k * P + P) for c in range(DC)],
                                [(rw_hi[:, layer, c * NL:c * NL + NL], rw_lo[:, layer, c * NL:c * NL + NL])
                                 for c in range(DC)])
                last.then_inc(s["logits"], 1)
                pe.wait_ge(s["cw"], 1)
                for k in range(NB):
                    dst = bank[3 + k // 8][0:3 * NCW, :].bitcast(BF16)[:, k % 8 * P:k % 8 * P + P]
                    pe.transpose(dst, cw3[:, k, :], identb[:]).then_inc(s["cwT"], 1)

            def gate_up(layer, n, blk, slot, round_, par, first, fresh):
                f = ffn[layer]
                if fresh:
                    pe.wait_ge(f["w_lo"], fresh[0] + 1)
                    pe.wait_ge(sel_ok[layer][slot], 16 * (round_ + 1))
                x4 = [xT(c, blk * BLK, blk * BLK + BLK) for c in range(DC)]
                if not first:
                    pe.wait_ge(f["silu"], n - 1)
                mm3c(bank[par][:, :], [(w_hi[:, slot, c * P:c * P + P], w_lo[:, slot, c * P:c * P + P])
                                       for c in range(DC)], x4).then_inc(f["g"], 1)
                if not first:
                    pe.wait_ge(f["gu"], n - 1)
                mm3c(bank[2 + par][:, :], [(w_hi[:, slot, (DC + c) * P:(DC + c) * P + P],
                                            w_lo[:, slot, (DC + c) * P:(DC + c) * P + P])
                                           for c in range(DC)], x4).then_inc(f["u"], 1)
                if not first:
                    pe.wait_ge(f["h"], n - 1)
                pe.matmul(bank[4 + par][:, :], sel[:, slot, :], cwT[:, blk * BLK:blk * BLK + BLK],
                          start=True, stop=True).then_inc(f["c"], 1)

            def down(layer, n, slot, par, opens, closes, unit, first):
                f = ffn[layer]
                pe.wait_ge(f["h_lo"], n + 1)
                if opens and not first:
                    pe.wait_ge(f["summed"], unit)
                for c in range(DC):
                    a = WGU + c * P
                    last = mm3(pair_bank[:, c, :], (w_hi[:, slot, a:a + P], w_lo[:, slot, a:a + P]),
                               (h_hi[:, par, :], h_lo[:, par, :]), start=opens, stop=closes)
                last.then_inc(f["down"], 1)

            def experts(layer):
                f = ffn[layer]
                n_loop, left = pairs_of(layer)
                pe.wait_ge(rout[layer]["turned"], 2)
                gate_up(layer, 0, 0, 0, 0, 0, True, (0,))

                def body(i, first, last):
                    for k in range(4 * NBLK):
                        n = i * 4 * NBLK + k
                        k1 = k + 1
                        if k1 < 4 * NBLK:
                            q, m = k1 // (2 * NBLK), k1 % (2 * NBLK)
                            slot = 2 * q + m % 2
                            gate_up(layer, n + 1, m // 2, slot, i, k1 % 2, first and k1 < 2,
                                    (i * SLOTS + slot,) if m < 2 else None)
                        elif not last or left:
                            gate_up(layer, n + 1, 0, 0, i + 1, 0, False, (i * SLOTS + SLOTS,))
                        q, m = k // (2 * NBLK), k % (2 * NBLK)
                        down(layer, n, 2 * q + m % 2, k % 2, m % 2 == 0, m % 2 == 1,
                             i * 2 * NBLK + k // 2, first and k == 0)

                body(0, True, False)
                with pe.Fori(1, n_loop - 1) as i:
                    body(i, False, False)
                body(n_loop - 1, False, True)
                for m in range(left * NBLK):
                    n = n_loop * 4 * NBLK + m
                    if m + 1 < left * NBLK:
                        gate_up(layer, n + 1, m + 1, 0, n_loop, (m + 1) % 2, False, None)
                    down(layer, n, 0, m % 2, True, True, n_loop * 2 * NBLK + m, False)

            def turn_sums(layer, g):
                f = ffn[layer]
                units = TILES[layer] // 2 * NBLK + (TILES[layer] % 2) * NBLK
                pe.wait_ge(f["summed"], units)
                for k in range(PER * g, PER * g + PER):
                    if k >= 2:
                        pe.wait_ge(f["x"], k - 1)
                    for c in range(DC):
                        last = pe.transpose(bank[2 + k % 2][:, c * P:c * P + P], accT[:, c, k * P:k * P + P],
                                            ident[:])
                    last.then_inc(f["turned"], 1)

            for k in range(NB):
                turn_rows(1, k)
            router(0)
            experts(0)
            for g in range(NBLK + 1):
                if g < NBLK:
                    turn_sums(0, g)
                if g >= 1:
                    for k in range(PER * g - PER, PER * g):
                        turn_rows(2, k)

            def wqkv(j, c, a, b):
                o = (j * DC + c) * D
                return (qkv_hi[:, o + a:o + b], qkv_lo[:, o + a:o + b])

            def project(B):
                for j in range(2 * DC):
                    n = 2 * DC * B + j
                    if n >= 2:
                        pe.wait_ge(a1["proj_sb"], n - 1)
                    a = j % DC * P
                    mm3c(bank[j % 2][:, :], [wqkv(j // DC, c, a, a + P) for c in range(DC)],
                         [xT(c, B * BLK, B * BLK + BLK) for c in range(DC)]).then_inc(a1["proj"], 1)

            def values(b):
                if b >= 1:
                    pe.wait_ge(a1["v_sb"], b)
                mm3c(bank[2][:, 0:D], [xT(c, b * P, b * P + P) for c in range(DC)],
                     [wqkv(2, c, 0, D) for c in range(DC)]).then_inc(a1["v"], 1)

            def scores1(b):
                B, o = b // PER, b % PER * P
                pe.wait_ge(a1["proj_sb"], 2 * DC * (B + 1))
                if b >= 1:
                    pe.wait_ge(a1["sm"], b)
                for c in range(DC):
                    last = pe.matmul(bank[3][:, 0:P], QT[B % 2][:, c, o:o + P], KT[B % 2][:, c, o:o + P],
                                     start=c == 0, stop=c == DC - 1)
                last.then_inc(a1["sc"], 1)

            def turn_p1(b):
                pe.wait_ge(a1["exp"], b + 1)
                if b >= 1:
                    pe.wait_ge(a1["pT_sb"], b)
                pe.transpose(bank[4][:, 0:P], pr[b % 2], ident[:]).then_inc(a1["pT"], 1)

            def weigh1(b):
                pe.wait_ge(a1["pT_sb"], b + 1)
                pe.wait_ge(a1["v_sb"], b + 1)
                if b >= 1:
                    pe.wait_ge(a1["t"], b)
                pe.matmul(bank[5][:, 0:D], prT[b % 2], V_sb[b % 2], start=True, stop=True).then_inc(a1["o"], 1)

            pe.wait_ge(qkv_lo_ok, 1)
            pe.wait_ge(norm[2]["lo"], NB)
            project(0)
            for i in range(NB + 2):
                if i < NB:
                    values(i)
                if i % PER == 2 and i // PER + 1 < NBLK:
                    project(i // PER + 1)
                if i < NB:
                    scores1(i)
                if 0 <= i - 1 < NB:
                    turn_p1(i - 1)
                    weigh1(i - 1)

            for k in range(NB):
                turn_rows(3, k)
            router(1)
            experts(1)
            for g in range(NBLK):
                turn_sums(1, g)


def _tiles(gate, up, down, np):
    n = gate.shape[0] // P

    def turned(w):
        return w.reshape(n, P, DC, P).transpose(0, 3, 2, 1).reshape(n, P, DC * P)

    return np.ascontiguousarray(np.concatenate([turned(gate), turned(up), down.reshape(n, P, D)], axis=2))


def _selectors(width, np, dt):
    n = TILES[0] if width == P else TILES[1]
    s = np.zeros((n, 3, NCW, P), np.float32)
    for t in range(n):
        for j in range(P):
            s[t, :, min((t * P + j) // width, NE), j] = 1.0
    return np.ascontiguousarray(s.reshape(n, 3 * NCW, P)).astype(dt)


def kernel(**inputs):
    import numpy as np
    import concourse.bacc as _bacc
    from concourse import mybir as _mybir
    from concourse.bass_utils import run_bass_kernel_spmd as _run

    a = {k: np.asarray(v) for k, v in inputs.items()}
    c = np.ascontiguousarray

    def wide(v):
        return c(np.broadcast_to(v.reshape(1, -1), (P, v.size)))

    def chunks(w):
        return w.T.reshape(DC, P, -1).transpose(1, 0, 2)

    def router_cols(w):
        return np.concatenate([w, np.zeros((NL - w.shape[0], D), w.dtype)])

    g0 = np.concatenate([a["L0_ffn_Wg"].transpose(0, 2, 1).reshape(-1, D), a["L0_ffn_sWg"].T])
    u0 = np.concatenate([a["L0_ffn_Wu"].transpose(0, 2, 1).reshape(-1, D), a["L0_ffn_sWu"].T])
    d0 = np.concatenate([a["L0_ffn_Wd"].reshape(-1, D), a["L0_ffn_sWd"]])
    egu, sgu = a["L1_ffn_expert_gate_up"], a["L1_ffn_shared_gate_up"]
    I, SI = egu.shape[1] // 2, sgu.shape[0] // 2
    pad = np.zeros((TILES[1] * P - NE * I - SI, D), egu.dtype)
    g1 = np.concatenate([egu[:, :I].reshape(-1, D), sgu[:SI], pad])
    u1 = np.concatenate([egu[:, I:].reshape(-1, D), sgu[SI:], pad])
    d1 = np.concatenate([a["L1_ffn_expert_down"].transpose(0, 2, 1).reshape(-1, D), a["L1_ffn_shared_down"].T, pad])
    import ml_dtypes
    bf16 = ml_dtypes.bfloat16
    arrays = {
        "x_in": c(a["x"]),
        "ctx_in": c(a["ctx_2048"]),
        "mask_in": c(a["mask_BxSxS2_ff0"]),
        "gates_in": wide(np.concatenate([a["g_xattn"], a["g_ffn"]])),
        "ident_in": np.eye(P, dtype=np.float32),
        "identb_in": np.eye(P, dtype=np.float32).astype(bf16),
        "lat_w": c(np.stack([a["L0_xattn_theta_w"].T, a["L0_xattn_phi_w"].T, a["L0_xattn_g_w"].T], axis=1)),
        "lat_b": c(np.stack([a["L0_xattn_theta_b"], a["L0_xattn_phi_b"], a["L0_xattn_g_b"]], axis=1)),
        "lat_out_w": c(a["L0_xattn_out_w"].T),
        "lat_out_b": c(a["L0_xattn_out_b"].reshape(P, 1)),
        "lat_norm": c(np.stack([a["L0_xattn_ln_gamma"], a["L0_xattn_ln_beta"]], axis=1)),
        "qkv_w": c(np.stack([chunks(a[f"L1_xattn_W{n}"]) for n in "qkv"], axis=1).reshape(P, -1)),
        "qk_b": c(np.stack([a[f"L1_xattn_b{n}"].reshape(DC, P).T for n in "qk"], axis=1)),
        "v_b": wide(a["L1_xattn_bv"]),
        "router_w": c(np.stack([chunks(router_cols(a["L0_ffn_Wr"])).reshape(P, -1),
                                chunks(router_cols(np.concatenate([a["L1_ffn_gate_w"],
                                                                   a["L1_ffn_shared_gate_vec"]]))).reshape(P, -1)],
                               axis=1)),
        "router_b": wide(a["L0_ffn_bias"]),
        "ffn_w0": _tiles(g0, u0, d0, np),
        "ffn_w1": _tiles(g1, u1, d1, np),
        "sel_in0": _selectors(P, np, bf16),
        "sel_in1": _selectors(I, np, bf16),
    }
    nc = _bacc.Bacc("TRN2", target_bir_lowering=False, num_devices=1)
    ap = {n: nc.dram_tensor(n, v.shape, _mybir.dt.from_np(v.dtype), kind="ExternalInput").ap()
          for n, v in arrays.items()}
    out = nc.dram_tensor("out", (NB, P, D), _mybir.dt.float32, kind="ExternalOutput").ap()
    pairs = {"ffn_w": [ap.pop("ffn_w0"), ap.pop("ffn_w1")], "sel_in": [ap.pop("sel_in0"), ap.pop("sel_in1")]}
    gated_blocks(nc, out=out, **pairs, **ap)
    r = _run(nc, [arrays], core_ids=[0])
    return r.results[0]["out"]
```

```python
from contextlib import ExitStack

import concourse.bass as bass
from concourse import mybir

F32 = mybir.dt.float32
F32R = mybir.dt.float32r
ALU = mybir.AluOpType
ACT = mybir.ActivationFunctionType
AX_X = mybir.AxisListType.X

P = 128
NB, D = 16, 256
DC = D // P
LAT = 64
BLK = 512
NBLK = NB * P // BLK
PER = BLK // P
NE = 16
NCW = NE + 1
NL = NCW + 1
NSENT = 8
GRAIN = 16
WGU, WD = 2 * DC * P, D
WT = WGU + WD
TILES = (17, 28)
TOPK = (2, 4)
TOPK_EPS = 1e-9
LN_EPS = 1e-5
EXPERT = (P, 176)
SLOTS = 4


def gated_blocks(nc, x_in, ctx_in, mask_in, gates_in, ident_in,
                 lat_w, lat_b, lat_out_w, lat_out_b, lat_norm,
                 qkv_w, qk_b, v_b, router_w, router_b, ffn_w, out):
    with ExitStack() as ctx:
        def sb(name, shape, dt=F32):
            return ctx.enter_context(nc.sbuf_tensor(name, shape, dt))

        def sem(name):
            return ctx.enter_context(nc.semaphore(name))

        x = sb("x", [P, NB, D])
        xn_comb = sb("xn_comb", [P, NB * D])
        xn = xn_comb[:, :].rearrange("p (b d) -> p b d", b=NB)
        comb = xn_comb[:, :].rearrange("p (b j n) -> p b j n", b=NBLK, j=2)
        xT_hi = sb("xT_hi", [P, DC, NB * P], F32R)
        xT_lo = sb("xT_lo", [P, DC, NB * P], F32R)
        ctx_accT = sb("ctx_accT", [P, NB * D])
        ctx_sb = ctx_accT[:, :].rearrange("p (b d) -> p b d", b=NB)
        accT = ctx_accT[:, :].rearrange("p (c n) -> p c n", c=DC)
        mask = sb("mask", [P, NB, P])
        ident = sb("ident", [P, P])
        tg = sb("tg", [P, 4])
        mhalf = sb("mhalf", [P, NB])
        ones = sb("ones", [LAT, LAT])
        bn6 = sb("bn6", [P, NB, 6])
        mv = sb("mv", [P, NB, 2])
        ve = sb("ve", [P, NB])
        rstd = sb("rstd", [P, NB])
        lw = sb("lw", [P, 3, LAT])
        lb = sb("lb", [LAT, 3])
        low = sb("low", [LAT, P])
        lob = sb("lob", [P, 1])
        lnorm = sb("lnorm", [LAT, 2, D])
        shared_bufs = sb("shared_bufs", [P, 6656])
        at = [0]

        def part(n, rows=P):
            a = at[0]
            at[0] += n
            return shared_bufs[0:rows, a:a + n]

        thph = [part(2 * D, LAT).rearrange("p (a t) -> p a t", a=2) for _ in range(2)]
        g_sb = [part(2 * LAT) for _ in range(4)]
        txT = [part(2 * LAT) for _ in range(2)]
        p_sb = [part(2 * D).rearrange("p (c s) -> p c s", c=2) for _ in range(2)]
        pT_sb = [part(2 * D) for _ in range(2)]
        tx = [part(D, LAT) for _ in range(4)]
        hu = [part(D, LAT) for _ in range(2)]
        hv = [part(D, LAT) for _ in range(2)]
        hr = [part(D, LAT) for _ in range(2)]
        assert at[0] <= 6656
        at[0] = 0
        QT = [part(DC * BLK).rearrange("p (c n) -> p c n", c=DC) for _ in range(2)]
        KT = [part(DC * BLK).rearrange("p (c n) -> p c n", c=DC) for _ in range(2)]
        V_sb = [part(D) for _ in range(4)]
        sm = [part(P) for _ in range(2)]
        pr = [part(P) for _ in range(2)]
        prT = [part(P) for _ in range(2)]
        assert at[0] <= 6656
        nmx = sb("nmx", [P, 2, 2])
        rs = sb("rs", [P, 4, 2])
        rr = sb("rr", [P, 2, 2])
        tx6 = sb("tx6", [LAT, 2, 6])
        txmv = sb("txmv", [LAT, 2, 2])
        mu = sb("mu", [LAT, 4, 1])
        dmu = sb("dmu", [LAT, 2, 1])
        q2 = sb("q2", [LAT, 2, 1])
        hve = sb("hve", [LAT, 2, 1])
        hrstd = sb("hrstd", [LAT, 2, 1])
        qkv_raw = sb("qkv_raw", [P, 3 * DC * D])
        qkv_hi = sb("qkv_hi", [P, 3 * DC * D], F32R)
        qkv_lo = sb("qkv_lo", [P, 3 * DC * D], F32R)
        qkb = sb("qkb", [P, 2, DC])
        vb = sb("vb", [P, D])
        nmx1 = sb("nmx1", [P, 2, 1])
        rs1 = sb("rs1", [P, 4, 1])
        rr1 = sb("rr1", [P, 2, 1])
        rt1 = sb("rt1", [P, 2, 1])
        rw_raw = sb("rw_raw", [P, 2, DC * NL])
        rw_hi = sb("rw_hi", [P, 2, DC * NL], F32R)
        rw_lo = sb("rw_lo", [P, 2, DC * NL], F32R)
        rb = sb("rb", [P, NE])
        z = sb("z", [P, PER, NCW])
        ez = sb("ez", [P, PER, NE])
        es = sb("es", [P, PER])
        rowst = sb("rowst", [P, PER])
        rowrc = sb("rowrc", [P, PER])
        probs = sb("probs", [P, PER, NE + NSENT])
        rest = sb("rest", [P, PER, NE + NSENT])
        top8 = sb("top8", [P, PER, 8])
        cw = sb("cw", [P, PER, NCW])
        cwT = sb("cwT", [NCW, 2, BLK])
        cw_rows = [nc.dram_tensor("cw_rows0", (NCW, NB * P), F32, kind="Internal").ap(),
                   nc.dram_tensor("cw_rows1", (TILES[1] * P // GRAIN, NB * P), F32, kind="Internal").ap()]
        w_raw = sb("w_raw", [P, SLOTS, WT])
        w_hi = sb("w_hi", [P, SLOTS, WT], F32R)
        w_lo = sb("w_lo", [P, SLOTS, WT], F32R)
        sg = sb("sg", [P, 2, BLK])
        gu = sb("gu", [P, BLK])
        hh = sb("hh", [P, 2, BLK])
        h_hi = sb("h_hi", [P, 2, BLK], F32R)
        h_lo = sb("h_lo", [P, 2, BLK], F32R)

        bank = [ctx.enter_context(nc.psum_tensor(f"bank{i}", [P, BLK], F32)) for i in range(6)]
        pair_bank = ctx.enter_context(nc.psum_tensor("pair_bank", [P, DC, BLK], F32))
        bank += [pair_bank[:, c, :] for c in range(DC)]

        x_in_ok = [sem(f"x_in_ok{g}") for g in range(NBLK)]
        small_ok, later_ok, out_ok = sem("small_ok"), sem("later_ok"), sem("out_ok")
        ctx_ok = [sem(f"ctx_ok{g}") for g in range(NBLK)]
        tanh_ok, const_ok, rw_hi_ok, rw_lo_ok = sem("tanh_ok"), sem("const_ok"), sem("rw_hi_ok"), sem("rw_lo_ok")
        qkv_hi_ok, qkv_lo_ok = sem("qkv_hi_ok"), sem("qkv_lo_ok")
        N_SMALL = 9

        names = ("stats", "aggr", "var", "rstd", "xn", "xTp", "hi", "lo")
        norm = [dict(zip(names, (sem(f"norm{n}_{s}") for s in names))) for n in range(4)]
        names = ("logits", "z", "centred", "exp", "step", "cw", "cwT", "turned", "stored")
        rout = [dict(zip(names, (sem(f"router{n}_{s}") for s in names))) for n in range(2)]
        names = ("w_hi", "w_lo", "g", "u", "silu", "gu", "h", "h_hi", "h_lo", "down", "summed", "zero",
                 "turned", "x")
        ffn = [dict(zip(names, (sem(f"ffn{n}_{s}") for s in names))) for n in range(2)]
        raw_ok = [[sem(f"raw{n}_ok{s}") for s in range(SLOTS)] for n in range(2)]
        comb_ok = [[sem(f"comb{n}_ok{b}") for b in range(NBLK)] for n in range(2)]
        names = ("thph", "thph_sb", "g_sb", "sc", "max", "exp", "rec", "pT", "pT_sb", "txT", "txT_sb", "tx",
                 "tx_sb", "st", "ag", "means", "mu", "d", "q", "var", "rstd", "u", "v", "h", "w", "ctx", "res", "x")
        a0 = dict(zip(names, (sem(f"lat_{s}") for s in names)))
        names = ("vb", "proj", "proj_sb", "v", "v_sb", "sc", "sm", "max", "exp", "rec", "rt", "pT", "pT_sb", "o",
                 "res", "x")
        a1 = dict(zip(names, (sem(f"att_{s}") for s in names)))

        block = ctx.enter_context(nc.Block())

        def rounds_of(layer):
            n = TILES[layer] // SLOTS
            assert TILES[layer] - SLOTS * n <= 1
            return (n, TILES[layer] - SLOTS * n)

        def pair_done(round_, slot):
            return (round_ * 2 + slot // 2 - 1) * 2 * NBLK

        def run(steps, *stages):
            for i in range(steps):
                for lag, stage in stages:
                    if 0 <= i - lag < NB:
                        stage(i - lag)

        def last_of_block(b):
            return b % PER == PER - 1

        A_STEPS = NB + 14
        LOAD, NORM, LATENTS, SCORES, TURN_P, WEIGH, TURN_TX, MEAN, VAR, OUT = 0, 1, 2, 3, 4, 5, 6, 7, 8, 9
        STATS, XN, TURN_X, LOGITS, TURN_CW = 9, 10, 11, 12, 14
        B_STEPS = NB + 22
        B_SUMS, B_XN, B_TURN, B_PROJ, B_SCORES, B_TURN_P, B_OUT = 0, 1, 2, 3, 10, 11, 12
        B_XN3, B_TURN3, B_LOGITS, B_TURN_CW = 13, 14, 15, 17

        @block.sync
        def _(sp):
            for g in range(NBLK):
                sp.dma_start(x[:, PER * g:PER * g + PER, :],
                             x_in[PER * g:PER * g + PER].rearrange("b p d -> p b d")).then_inc(x_in_ok[g], 16)
                if g == 0:
                    small = [(gates_in, tg), (ident_in, ident), (lat_w, lw), (lat_b, lb), (lat_out_w, low),
                             (lat_out_b, lob), (lat_norm, lnorm), (router_w, rw_raw), (router_b, rb)]
                    assert len(small) == N_SMALL
                    for src, dst in small:
                        sp.dma_start(dst[:], src).then_inc(small_ok, 16)
                sp.dma_start(ctx_sb[:, PER * g:PER * g + PER, :],
                             ctx_in[PER * g:PER * g + PER].rearrange("b p d -> p b d")).then_inc(ctx_ok[g], 16)
            for src, dst in [(qkv_w, qkv_raw[:]), (qk_b, qkb[:]), (v_b, vb[:]),
                             (mask_in.rearrange("b p k -> p b k"), mask[:])]:
                sp.dma_start(dst, src).then_inc(later_ok, 16)

            def load_tile(layer, t, slot):
                if not (isinstance(t, int) and t < SLOTS):
                    sp.wait_ge(ffn[layer]["w_lo"], t - SLOTS + 1)
                elif layer == 1:
                    sp.wait_ge(ffn[0]["w_lo"], TILES[0])
                sp.dma_start(w_raw[:, slot, :], ffn_w[layer][t]).then_inc(raw_ok[layer][slot], 16)

            def load_comb(layer, t, blk, j):
                cols = slice(blk * BLK, blk * BLK + BLK)
                if layer == 0:
                    src = cw_rows[0][t, cols].unsqueeze(0).to_broadcast([P, BLK])
                    sp.dma_start(comb[:, blk, j, :], src).then_inc(comb_ok[0][blk], 16)
                else:
                    src = cw_rows[1].rearrange("(t g) n -> t g n", g=P // GRAIN)[t][:, cols]
                    sp.dma_start(comb[:, blk, j, :],
                                 src.unsqueeze(1).to_broadcast([P // GRAIN, GRAIN, BLK]))\
                        .then_inc(comb_ok[1][blk], 16)

            for layer in range(2):
                f, r = ffn[layer], rout[layer]
                for t in range(SLOTS):
                    load_tile(layer, t, t)
                for g in range(NBLK):
                    sp.wait_ge(r["turned"], g + 1)
                    cols = slice(g * BLK, g * BLK + BLK)
                    if layer == 0:
                        sp.dma_start(cw_rows[0][:, cols], cwT[:, g % 2, :]).then_inc(r["stored"], 16)
                        stored = 16
                    else:
                        n = EXPERT[1] // GRAIN
                        sp.dma_start(cw_rows[1][0:NE * n, cols].rearrange("(e r) n -> e r n", r=n),
                                     cwT[0:NE, g % 2, :].unsqueeze(1).to_broadcast([NE, n, BLK]))\
                            .then_inc(r["stored"], 16)
                        n = TILES[1] * P // GRAIN - NE * n
                        sp.dma_start(cw_rows[1][NE * EXPERT[1] // GRAIN:, cols].unsqueeze(0),
                                     cwT[NE:NCW, g % 2, :].unsqueeze(1).to_broadcast([1, n, BLK]))\
                            .then_inc(r["stored"], 16)
                        stored = 32
                    sp.wait_ge(r["stored"], stored * (g + 1))
                    sp.wait_ge(norm[1 + 2 * layer]["lo"], PER * g + PER)
                    for j in range(2):
                        load_comb(layer, j, g, j)
                n_round, left = rounds_of(layer)

                def body(i, last):
                    for q in range(2):
                        for b in range(NBLK):
                            more = 2 if not last or q == 0 else left
                            if b == 0 and not last:
                                for j in range(2):
                                    load_tile(layer, i * SLOTS + SLOTS + 2 * q + j, 2 * q + j)
                            elif b == 0 and q == 0 and left:
                                load_tile(layer, n_round * SLOTS, 0)
                            if more:
                                sp.wait_ge(f["h"], i * 4 * NBLK + (q * NBLK + b) * 2 + 2)
                            for j in range(more):
                                load_comb(layer, i * SLOTS + 2 * q + 2 + j, b, j)

                body(0, False)
                with sp.Fori(1, n_round - 1) as i:
                    body(i, False)
                body(n_round - 1, True)
            for k in range(NB):
                sp.wait_ge(ffn[1]["x"], k + 1)
                sp.dma_start(out[k], x[:, k, :]).then_inc(out_ok, 16)
            sp.wait_ge(out_ok, 16 * NB)

        @block.gpsimd
        def _(pool):
            pool.memset(mhalf[:], -0.5).then_inc(const_ok, 1)
            pool.memset(ones[:], 1.0 / LAT).then_inc(const_ok, 1)
            pool.memset(probs[:], -1.0).then_inc(const_ok, 1)
            pool.wait_ge(const_ok, 3)
            pool.wait_ge(small_ok, 16 * N_SMALL)
            pool.wait_ge(tanh_ok, 1)

            def row_rstd(n):
                def stage(b):
                    pool.wait_ge(norm[n]["var"], b + 1)
                    pool.tensor_tensor(rstd[:, b:b + 1], ve[:, b:b + 1], mhalf[:, 0:1], ALU.pow)\
                        .then_inc(norm[n]["rstd"], 1)
                return stage

            def add_context(b):
                pool.wait_ge(norm[0]["xn"], b + 1)
                pool.wait_ge(ctx_ok[b // PER], 16)
                pool.wait_ge(a0["thph"], b + 1)
                pool.tensor_scalar(ctx_sb[:, b, :], ctx_sb[:, b, :], lob[:, 0:1], tg[:, 0:1], ALU.add, ALU.mult)\
                    .then_inc(a0["ctx"], 1)
                pool.wait_ge(a0["ctx"], b + 1)
                pool.tensor_tensor(x[:, b, :], x[:, b, :], ctx_sb[:, b, :], ALU.add).then_inc(a0["res"], 1)

            def lat_rstd(b):
                pool.wait_ge(a0["var"], b + 1)
                pool.tensor_tensor(hrstd[:, b % 2, :], hve[:, b % 2, :], mhalf[0:LAT, 0:1], ALU.pow)\
                    .then_inc(a0["rstd"], 1)

            run(A_STEPS, (VAR, lat_rstd), (STATS, row_rstd(1)), (LATENTS, add_context), (LOAD, row_rstd(0)))
            pool.wait_ge(a0["x"], NB)
            pool.memset(ctx_accT[:], 0.0).then_inc(ffn[0]["zero"], 1)
            pool.wait_ge(later_ok, 16 * 4)
            pool.tensor_scalar(vb[:], vb[:], tg[:, 1:2], None, ALU.mult).then_inc(a1["vb"], 1)
            pool.wait_ge(a1["vb"], 1)

            def add_v_bias(b):
                pool.wait_ge(norm[2]["xn"], b + 1)
                pool.tensor_tensor(x[:, b, :], x[:, b, :], vb[:], ALU.add).then_inc(a1["res"], 1)

            run(B_STEPS, (B_SUMS, row_rstd(2)), (B_XN, add_v_bias), (B_OUT, row_rstd(3)))
            pool.wait_ge(ffn[0]["turned"], NB)
            pool.memset(ctx_accT[:], 0.0).then_inc(ffn[1]["zero"], 1)

        @block.scalar
        def _(act):
            act.wait_ge(small_ok, 16 * N_SMALL)
            act.activation(tg[:], tg[:], ACT.Tanh).then_inc(tanh_ok, 1)
            act.activation(rw_hi[:], rw_raw[:], ACT.Copy).then_inc(rw_hi_ok, 1)

            def split_rows(n, src):
                def stage(k):
                    act.wait_ge(norm[n]["xTp"], k + 1)
                    act.activation(xT_hi[:, :, k * P:k * P + P],
                                   bank[src][:, 0:D].rearrange("p (c n) -> p c n", c=DC),
                                   ACT.Copy).then_inc(norm[n]["hi"], 1)
                return stage

            def router_exp(layer):
                def stage(b):
                    if last_of_block(b):
                        g, s = b // PER, rout[layer]
                        act.wait_ge(s["centred"], g + 1)
                        act.activation(ez[:], z[:, :, 0:NE], ACT.Exp).then_inc(s["exp"], 1)
                        if layer == 1:
                            act.activation(es[:], z[:, :, NE], ACT.Exp, scale=-1.0).then_inc(s["exp"], 1)
                return stage

            def router_out(layer, src):
                def stage(b):
                    if last_of_block(b):
                        g, s = b // PER, rout[layer]
                        act.wait_ge(s["cwT"], g + 1)
                        if g >= 2:
                            act.wait_ge(s["stored"], (16, 32)[layer] * (g - 1))
                        act.activation(cwT[:, g % 2, :], bank[src][0:NCW, :], ACT.Copy).then_inc(s["turned"], 1)
                return stage

            def latents_out(b):
                act.wait_ge(a0["thph"], b + 1)
                if b >= 2:
                    act.wait_ge(a0["sc"], b - 1)
                for j in range(2):
                    act.activation(thph[b % 2][:, j, :], bank[0][0:LAT, j * D:j * D + D], ACT.Identity,
                                   bias=lb[:, j:j + 1]).then_inc(a0["thph_sb"], 1)
                if b >= 4:
                    act.wait_ge(a0["txT"], b - 3)
                act.activation(g_sb[b % 4], bank[1][:, 0:2 * LAT], ACT.Copy).then_inc(a0["g_sb"], 1)

            def exps(b):
                act.wait_ge(a0["max"], b + 1)
                if b >= 2:
                    act.wait_ge(a0["pT"], b - 1)
                if b >= 4:
                    act.wait_ge(a0["rec"], b - 3)
                for c in range(2):
                    act.activation(p_sb[b % 2][:, c, :], bank[2][:, c * D:c * D + D], ACT.Exp,
                                   bias=nmx[:, b % 2, c:c + 1], accum_out=rs[:, b % 4, c:c + 1])\
                        .then_inc(a0["exp"], 1)

            def pT_out(b):
                act.wait_ge(a0["pT"], b + 1)
                if b >= 2:
                    act.wait_ge(a0["txT"], b - 1)
                act.activation(pT_sb[b % 2], bank[3][:, :], ACT.Copy).then_inc(a0["pT_sb"], 1)

            def tx_out(b):
                act.wait_ge(a0["tx"], b + 1)
                if b >= 4:
                    act.wait_ge(a0["u"], b - 3)
                act.activation(tx[b % 4], bank[5][0:LAT, 0:D], ACT.Identity, bias=lb[:, 2:3])\
                    .then_inc(a0["tx_sb"], 1)

            def relu(b):
                act.wait_ge(a0["v"], b + 1)
                if b >= 2:
                    act.wait_ge(a0["w"], b - 1)
                act.activation(hr[b % 2], hv[b % 2], ACT.Relu).then_inc(a0["h"], 1)

            run(A_STEPS, (TURN_P, pT_out), (SCORES, exps), (TURN_TX, tx_out), (TURN_X, split_rows(1, 4)),
                (LATENTS, latents_out), (VAR, relu), (LOGITS, router_exp(0)), (TURN_CW, router_out(0, 1)))

            def split_tile(layer, t, slot, round_):
                f = ffn[layer]
                act.wait_ge(raw_ok[layer][slot], 16 * (round_ + 1))
                if not (isinstance(t, int) and t < SLOTS):
                    act.wait_ge(f["down"], pair_done(round_, slot))
                elif layer == 1:
                    act.wait_ge(ffn[0]["down"], TILES[0] * NBLK)
                act.activation(w_hi[:, slot, :], w_raw[:, slot, :], ACT.Copy).then_inc(f["w_hi"], 1)

            def hidden(layer, n, par, first):
                f = ffn[layer]
                act.wait_ge(f["g"], n + 1)
                if not first:
                    act.wait_ge(f["gu"], n - 1)
                act.activation(sg[:, par, :], bank[par][:, :], ACT.Silu).then_inc(f["silu"], 1)
                act.wait_ge(f["h"], n + 1)
                if not first:
                    act.wait_ge(f["down"], n - 1)
                act.activation(h_hi[:, par, :], hh[:, par, :], ACT.Copy).then_inc(f["h_hi"], 1)

            def experts(layer):
                n_round, left = rounds_of(layer)

                def body(i, last):
                    for q in range(2):
                        for m in range(2 * NBLK):
                            k = q * 2 * NBLK + m
                            hidden(layer, i * 4 * NBLK + k, m % 2, first=isinstance(i, int) and i == 0 and k < 2)
                            if m in (3, 5):
                                slot = (2 * q + 2 + (m == 5)) % SLOTS
                                if q == 0:
                                    split_tile(layer, i * SLOTS + slot, slot, i)
                                elif not last or slot < left:
                                    split_tile(layer, i * SLOTS + SLOTS + slot, slot, i + 1)

                body(0, False)
                with act.Fori(1, n_round - 1) as i:
                    body(i, False)
                body(n_round - 1, True)
                for m in range(left * NBLK):
                    hidden(layer, n_round * 4 * NBLK + m, m % 2, False)

            split_tile(0, 0, 0, 0)
            split_tile(0, 1, 1, 0)
            experts(0)

            act.wait_ge(later_ok, 16 * 4)
            act.activation(qkv_hi[:], qkv_raw[:], ACT.Copy).then_inc(qkv_hi_ok, 1)
            split_tile(1, 0, 0, 0)
            split_tile(1, 1, 1, 0)

            def proj_out(b):
                B, j = b // PER, b % PER
                act.wait_ge(a1["proj"], b + 1)
                if B >= 2:
                    act.wait_ge(a1["sc"], PER * (B - 1))
                act.activation((QT, KT)[j // DC][B % 2][:, j % DC, :], bank[j % 2][:, :], ACT.Identity,
                               bias=qkb[:, j // DC, j % DC:j % DC + 1]).then_inc(a1["proj_sb"], 1)

            def v_out(b):
                act.wait_ge(a1["v"], b + 1)
                if b >= 4:
                    act.wait_ge(a1["o"], b - 3)
                act.activation(V_sb[b % 4], bank[2][:, 0:D], ACT.Copy).then_inc(a1["v_sb"], 1)

            def exp1(b):
                act.wait_ge(a1["max"], b + 1)
                if b >= 2:
                    act.wait_ge(a1["pT"], b - 1)
                if b >= 4:
                    act.wait_ge(a1["rec"], b - 3)
                act.activation(pr[b % 2], sm[b % 2], ACT.Exp, bias=nmx1[:, b % 2, :],
                               accum_out=rs1[:, b % 4, :]).then_inc(a1["exp"], 1)

            def prT_out(b):
                act.wait_ge(a1["pT"], b + 1)
                if b >= 2:
                    act.wait_ge(a1["o"], b - 1)
                act.activation(prT[b % 2], bank[4][:, 0:P], ACT.Copy).then_inc(a1["pT_sb"], 1)

            run(B_STEPS, (B_TURN_P, prT_out), (B_SCORES, exp1), (B_PROJ + PER - 1, proj_out), (B_SCORES, v_out),
                (B_TURN, split_rows(2, 6)), (B_TURN3, split_rows(3, 7)), (B_LOGITS, router_exp(1)),
                (B_TURN_CW, router_out(1, 4)))
            experts(1)

        @block.vector
        def _(dve):
            dve.wait_ge(small_ok, 16 * N_SMALL)
            dve.wait_ge(rw_hi_ok, 1)
            dve.tensor_tensor(rw_lo[:], rw_raw[:], rw_hi[:].bitcast(F32), ALU.subtract).then_inc(rw_lo_ok, 1)
            dve.wait_ge(tanh_ok, 1)
            dve.wait_ge(const_ok, 3)

            def row_stats(n, ready):
                def stage(b):
                    s = norm[n]
                    ready(b)
                    dve.bn_stats(bn6[:, b, :], x[:, b, :]).then_inc(s["stats"], 1)
                    dve.wait_ge(s["stats"], b + 1)
                    dve.bn_aggr(mv[:, b, :], bn6[:, b, :]).then_inc(s["aggr"], 1)
                    dve.wait_ge(s["aggr"], b + 1)
                    dve.tensor_scalar(ve[:, b:b + 1], mv[:, b, 1:2], LN_EPS, None, ALU.add).then_inc(s["var"], 1)
                return stage

            def normalise(n):
                def stage(b):
                    s = norm[n]
                    dve.wait_ge(s["rstd"], b + 1)
                    dve.tensor_scalar(xn[:, b, :], x[:, b, :], mv[:, b, 0:1], rstd[:, b:b + 1],
                                      ALU.subtract, ALU.mult).then_inc(s["xn"], 1)
                return stage

            def split_rows(n, src):
                def stage(k):
                    dve.wait_ge(norm[n]["hi"], k + 1)
                    dst = slice(k * P, k * P + P)
                    dve.tensor_tensor(xT_lo[:, :, dst], bank[src][:, 0:D].rearrange("p (c n) -> p c n", c=DC),
                                      xT_hi[:, :, dst].bitcast(F32), ALU.subtract).then_inc(norm[n]["lo"], 1)
                return stage

            def router(layer):
                s = rout[layer]
                done = [0]

                def step(ins):
                    done[0] += 1
                    ins.then_inc(s["step"], 1)
                    dve.wait_ge(s["step"], done[0])

                def wide(v):
                    return v.unsqueeze(2).to_broadcast([P, PER, NE])

                def stage(b):
                    if not last_of_block(b):
                        return
                    g = b // PER
                    dve.wait_ge(s["logits"], g + 1)
                    if g >= 1:
                        dve.wait_ge(s["exp"], (1 + layer) * g)
                    lg = bank[(6, 4)[layer]][:, 128:128 + PER * NL].rearrange("p (b e) -> p b e", b=PER)
                    if layer == 0:
                        ins = dve.tensor_tensor(z[:, :, 0:NE], lg[:, :, 0:NE],
                                                rb[:].unsqueeze(1).to_broadcast([P, PER, NE]), ALU.add)
                    else:
                        ins = dve.tensor_copy(z[:], lg[:, :, 0:NCW])
                    ins.then_inc(s["z"], 1)
                    dve.wait_ge(s["z"], g + 1)
                    step(dve.tensor_reduce(rowst[:], z[:, :, 0:NE], AX_X, ALU.max))
                    dve.tensor_tensor(z[:, :, 0:NE], z[:, :, 0:NE], wide(rowst[:]), ALU.subtract)\
                        .then_inc(s["centred"], 1)
                    dve.wait_ge(s["exp"], (1 + layer) * (g + 1))
                    step(dve.tensor_reduce(rowst[:], ez[:], AX_X, ALU.add))
                    step(dve.reciprocal(rowrc[:], rowst[:]))
                    step(dve.tensor_tensor(probs[:, :, 0:NE], ez[:], wide(rowrc[:]), ALU.mult))
                    for k in range(PER):
                        last = dve.max(top8[:, k, :], probs[:, k, 0:NE])
                    step(last)
                    step(dve.memset(top8[:, :, TOPK[layer]:8], -1.0))
                    for k in range(PER):
                        last = dve.match_replace(rest[:, k, :], top8[:, k, :], probs[:, k, :], 0.0)
                    step(last)
                    step(dve.tensor_tensor(rest[:, :, 0:NE], probs[:, :, 0:NE], rest[:, :, 0:NE], ALU.subtract))
                    step(dve.tensor_reduce(rowst[:], rest[:, :, 0:NE], AX_X, ALU.add))
                    if layer == 0:
                        step(dve.tensor_scalar(rowst[:], rowst[:], TOPK_EPS, None, ALU.add))
                    step(dve.reciprocal(rowrc[:], rowst[:]))
                    if g >= 1:
                        dve.wait_ge(s["cwT"], g)
                    if layer == 0:
                        dve.memset(cw[:, :, NE:NCW], 1.0)
                    else:
                        step(dve.tensor_scalar(es[:], es[:], 1.0, None, ALU.add))
                        dve.reciprocal(cw[:, :, NE], es[:])
                    dve.tensor_tensor(cw[:, :, 0:NE], rest[:, :, 0:NE], wide(rowrc[:]), ALU.mult)\
                        .then_inc(s["cw"], 1)
                return stage

            def maxes(b):
                dve.wait_ge(a0["sc"], b + 1)
                if b >= 2:
                    dve.wait_ge(a0["exp"], 2 * (b - 1))
                dve.tensor_reduce(nmx[:, b % 2, :], bank[2][:, :].rearrange("p (c s) -> p c s", c=2), AX_X,
                                  ALU.max, negate=True).then_inc(a0["max"], 1)

            def sums(b):
                dve.wait_ge(a0["exp"], 2 * (b + 1))
                dve.reciprocal(rr[:, b % 2, :], rs[:, b % 4, :]).then_inc(a0["rec"], 1)

            def weigh_out(b):
                dve.wait_ge(a0["txT"], b + 1)
                dve.wait_ge(a0["rec"], b + 1)
                if b >= 2:
                    dve.wait_ge(a0["tx"], b - 1)
                dve.tensor_tensor(txT[b % 2].rearrange("p (c l) -> p c l", c=2),
                                  bank[4][:, 0:2 * LAT].rearrange("p (c l) -> p c l", c=2),
                                  rr[:, b % 2, :].unsqueeze(2).to_broadcast([P, 2, LAT]), ALU.mult)\
                    .then_inc(a0["txT_sb"], 1)

            def tx_stats(b):
                dve.wait_ge(a0["tx_sb"], b + 1)
                dve.bn_stats(tx6[:, b % 2, :], tx[b % 4]).then_inc(a0["st"], 1)
                dve.wait_ge(a0["st"], b + 1)
                if b >= 2:
                    dve.wait_ge(a0["means"], b - 1)
                dve.bn_aggr(txmv[:, b % 2, :], tx6[:, b % 2, :]).then_inc(a0["ag"], 1)

            def tx_mean(b):
                dve.wait_ge(a0["means"], b + 1)
                dve.tensor_copy(mu[:, b % 4, :], bank[6][0:LAT, 0:1]).then_inc(a0["mu"], 1)
                dve.wait_ge(a0["mu"], b + 1)
                dve.tensor_tensor(dmu[:, b % 2, :], txmv[:, b % 2, 0:1], mu[:, b % 4, :], ALU.subtract)\
                    .then_inc(a0["d"], 1)
                dve.wait_ge(a0["d"], b + 1)
                if b >= 2:
                    dve.wait_ge(a0["means"], b)
                dve.scalar_tensor_tensor(q2[:, b % 2, :], dmu[:, b % 2, :], dmu[:, b % 2, :],
                                         txmv[:, b % 2, 1:2], ALU.mult, ALU.add).then_inc(a0["q"], 1)

            def tx_var(b):
                dve.wait_ge(a0["means"], b + 2)
                if b >= 2:
                    dve.wait_ge(a0["rstd"], b - 1)
                dve.tensor_scalar(hve[:, b % 2, :], bank[6][0:LAT, 1:2], LN_EPS, None, ALU.add)\
                    .then_inc(a0["var"], 1)
                dve.scalar_tensor_tensor(hu[b % 2], tx[b % 4], mu[:, b % 4, :], lnorm[:, 0, :],
                                         ALU.subtract, ALU.mult).then_inc(a0["u"], 1)

            def tx_scaled(b):
                dve.wait_ge(a0["rstd"], b + 1)
                dve.wait_ge(a0["u"], b + 1)
                if b >= 2:
                    dve.wait_ge(a0["h"], b - 1)
                dve.scalar_tensor_tensor(hv[b % 2], hu[b % 2], hrstd[:, b % 2, :], lnorm[:, 1, :],
                                         ALU.mult, ALU.add).then_inc(a0["v"], 1)

            def lat_add(b):
                dve.wait_ge(a0["w"], b + 1)
                dve.wait_ge(a0["res"], b + 1)
                dve.scalar_tensor_tensor(x[:, b, :], bank[7][:, 0:D], tg[:, 0:1], x[:, b, :],
                                         ALU.mult, ALU.add).then_inc(a0["x"], 1)

            run(A_STEPS, (SCORES, maxes), (WEIGH, weigh_out), (MEAN, tx_mean), (VAR, tx_var),
                (TURN_X, split_rows(1, 4)), (TURN_TX, tx_stats), (OUT, lat_add), (VAR, tx_scaled),
                (STATS, row_stats(1, lambda b: dve.wait_ge(a0["x"], b + 1))), (XN, normalise(1)),
                (LOAD, row_stats(0, lambda b: dve.wait_ge(x_in_ok[b // PER], 16))), (SCORES, sums),
                (NORM, normalise(0)), (LOGITS, router(0)))

            def split_tile(layer, t, slot):
                f = ffn[layer]
                dve.wait_ge(f["w_hi"], t + 1)
                dve.tensor_tensor(w_lo[:, slot, :], w_raw[:, slot, :], w_hi[:, slot, :].bitcast(F32),
                                  ALU.subtract).then_inc(f["w_lo"], 1)

            def add_sum(layer, downs, blk):
                f = ffn[layer]
                dve.wait_ge(f["down"], downs)
                dst = accT[:, :, blk * BLK:blk * BLK + BLK]
                dve.tensor_tensor(dst, pair_bank[:], dst, ALU.add).then_inc(f["summed"], 1)

            def hidden(layer, n, par, first, comb_at, comb_count, between):
                f = ffn[layer]
                dve.wait_ge(f["silu"], n + 1)
                dve.wait_ge(f["u"], n + 1)
                if not (isinstance(n, int) and n == 0):
                    dve.wait_ge(f["h"], n)
                dve.tensor_tensor(gu[:], sg[:, par, :], bank[2 + par][:, :], ALU.mult).then_inc(f["gu"], 1)
                dve.wait_ge(f["gu"], n + 1)
                dve.wait_ge(comb_ok[layer][comb_at[0]], comb_count)
                if not first:
                    dve.wait_ge(f["h_lo"], n - 1)
                dve.tensor_tensor(hh[:, par, :], gu[:], comb[:, comb_at[0], comb_at[1], :], ALU.mult)\
                    .then_inc(f["h"], 1)
                between()
                dve.wait_ge(f["h_hi"], n + 1)
                dve.tensor_tensor(h_lo[:, par, :], hh[:, par, :], h_hi[:, par, :].bitcast(F32),
                                  ALU.subtract).then_inc(f["h_lo"], 1)

            def experts(layer):
                n_round, left = rounds_of(layer)
                dve.wait_ge(ffn[layer]["zero"], 1)

                def body(i, first, last):
                    for q in range(2):
                        for m in range(2 * NBLK):
                            k = q * 2 * NBLK + m

                            def between():
                                if m % 2 == 0 and not (first and k == 0):
                                    add_sum(layer, i * 4 * NBLK + k, (m // 2 - 1) % NBLK)

                            hidden(layer, i * 4 * NBLK + k, m % 2, first and k < 2, (m // 2, m % 2),
                                   i * 64 + (q + 1) * 32, between)
                            if m in (3, 5):
                                slot = (2 * q + 2 + (m == 5)) % SLOTS
                                if q == 0:
                                    split_tile(layer, i * SLOTS + slot, slot)
                                elif not last or slot < left:
                                    split_tile(layer, i * SLOTS + SLOTS + slot, slot)

                body(0, True, False)
                with dve.Fori(1, n_round - 1) as i:
                    body(i, False, False)
                body(n_round - 1, False, True)
                steps = n_round * 4 * NBLK
                for m in range(left * NBLK):
                    hidden(layer, steps + m, m % 2, False, (m, 0), n_round * 64 + 16,
                           lambda: add_sum(layer, steps + m, (m - 1) % NBLK))
                add_sum(layer, steps + left * NBLK, NBLK - 1)

            def add_ffn(layer, src):
                def stage(k):
                    f = ffn[layer]
                    dve.wait_ge(f["turned"], k + 1)
                    dve.scalar_tensor_tensor(x[:, k, :], bank[src(k)][:, 0:D], tg[:, 2 + layer:3 + layer],
                                             x[:, k, :], ALU.mult, ALU.add).then_inc(f["x"], 1)
                return stage

            split_tile(0, 0, 0)
            split_tile(0, 1, 1)
            experts(0)

            dve.wait_ge(qkv_hi_ok, 1)
            dve.tensor_tensor(qkv_lo[:], qkv_raw[:], qkv_hi[:].bitcast(F32), ALU.subtract).then_inc(qkv_lo_ok, 1)
            split_tile(1, 0, 0)
            split_tile(1, 1, 1)
            dve.wait_ge(later_ok, 16 * 4)

            def masked(b):
                dve.wait_ge(a1["sc"], b + 1)
                if b >= 2:
                    dve.wait_ge(a1["exp"], b - 1)
                dve.scalar_tensor_tensor(sm[b % 2], bank[3][:, 0:P], float(D) ** -0.5, mask[:, b, :],
                                         ALU.mult, ALU.add).then_inc(a1["sm"], 1)
                dve.wait_ge(a1["sm"], b + 1)
                dve.tensor_reduce(nmx1[:, b % 2, :], sm[b % 2], AX_X, ALU.max, negate=True).then_inc(a1["max"], 1)

            def att_scale(b):
                dve.wait_ge(a1["exp"], b + 1)
                dve.reciprocal(rr1[:, b % 2, :], rs1[:, b % 4, :]).then_inc(a1["rec"], 1)
                dve.wait_ge(a1["rec"], b + 1)
                dve.tensor_scalar(rt1[:, b % 2, :], rr1[:, b % 2, :], tg[:, 1:2], None, ALU.mult)\
                    .then_inc(a1["rt"], 1)

            def att_add(b):
                dve.wait_ge(a1["rt"], b + 1)
                dve.wait_ge(a1["o"], b + 1)
                dve.wait_ge(a1["res"], b + 1)
                dve.scalar_tensor_tensor(x[:, b, :], bank[5][:, 0:D], rt1[:, b % 2, :], x[:, b, :],
                                         ALU.mult, ALU.add).then_inc(a1["x"], 1)

            run(B_STEPS, (B_SUMS, add_ffn(0, lambda k: 6)),
                (B_SUMS, row_stats(2, lambda b: dve.wait_ge(ffn[0]["x"], b + 1))),
                (B_SCORES, masked), (B_XN, normalise(2)), (B_XN3, normalise(3)), (B_TURN_P, att_scale),
                (B_OUT, att_add), (B_OUT, row_stats(3, lambda b: dve.wait_ge(a1["x"], b + 1))),
                (B_TURN, split_rows(2, 6)), (B_TURN3, split_rows(3, 7)), (B_LOGITS, router(1)))
            experts(1)
            for k in range(NB):
                add_ffn(1, lambda k: 4 + k % 2)(k)

        @block.tensor
        def _(pe):
            def mm3(dst, w, xv, start=True, stop=True):
                pe.matmul(dst, w[0], xv[0], start=start, stop=False)
                pe.matmul(dst, w[0], xv[1], start=False, stop=False)
                return pe.matmul(dst, w[1], xv[0], start=False, stop=stop)

            def mm3c(dst, ws, xs):
                for c in range(len(ws)):
                    last = mm3(dst, ws[c], xs[c], start=c == 0, stop=c == len(ws) - 1)
                return last

            def xT(c, a, b):
                return (xT_hi[:, c, a:b], xT_lo[:, c, a:b])

            def turn_rows(n, dst, bank_free):
                def stage(k):
                    s = norm[n]
                    pe.wait_ge(s["xn"], k + 1)
                    if k >= 1:
                        pe.wait_ge(s["lo"], k)
                    bank_free(k)
                    for c in range(DC):
                        last = pe.transpose(bank[dst][:, c * P:c * P + P], xn[:, k, c * P:c * P + P], ident[:])
                    last.then_inc(s["xTp"], 1)
                return stage

            def turn_sums(layer, k, dst):
                for c in range(DC):
                    last = pe.transpose(bank[dst][:, c * P:c * P + P], accT[:, c, k * P:k * P + P], ident[:])
                last.then_inc(ffn[layer]["turned"], 1)

            def logits(layer, dst, bank_free):
                def stage(b):
                    if not last_of_block(b):
                        return
                    s = rout[layer]
                    pe.wait_ge(norm[1 + 2 * layer]["lo"], b + 1)
                    bank_free(b)
                    for k in range(b - PER + 1, b + 1):
                        o = 128 + k % PER * NL
                        last = mm3c(bank[dst][:, o:o + NL], [xT(c, k * P, k * P + P) for c in range(DC)],
                                    [(rw_hi[:, layer, c * NL:c * NL + NL], rw_lo[:, layer, c * NL:c * NL + NL])
                                     for c in range(DC)])
                    last.then_inc(s["logits"], 1)
                return stage

            def turn_weights(layer, dst, bank_free):
                def stage(b):
                    if not last_of_block(b):
                        return
                    s = rout[layer]
                    pe.wait_ge(s["cw"], b // PER + 1)
                    bank_free(b)
                    for k in range(PER):
                        last = pe.transpose(bank[dst][0:NCW, k * P:k * P + P], cw[:, k, :], ident[:])
                    last.then_inc(s["cwT"], 1)
                return stage

            def blocks_before(step, lag):
                return max(0, min(NBLK, (step - lag) // PER))

            def latents(b):
                pe.wait_ge(norm[0]["xn"], b + 1)
                if b % PER == 0:
                    pe.wait_ge(ctx_ok[b // PER], 16)
                if b >= 1:
                    pe.wait_ge(a0["thph_sb"], 2 * b)
                    pe.wait_ge(a0["g_sb"], b)
                if turned := blocks_before(b + LATENTS, TURN_CW):
                    pe.wait_ge(rout[0]["turned"], turned)
                pe.matmul(bank[0][0:LAT, 0:D], lw[:, 0, :], ctx_sb[:, b, :], start=True, stop=True)
                pe.matmul(bank[0][0:LAT, D:2 * D], lw[:, 1, :], xn[:, b, :], start=True, stop=True)
                for c in range(2):
                    last = pe.matmul(bank[1][:, c * LAT:c * LAT + LAT], xn[:, b, c * P:c * P + P], lw[:, 2, :],
                                     start=True, stop=True)
                last.then_inc(a0["thph"], 1)

            def scores(b):
                pe.wait_ge(a0["thph_sb"], 2 * (b + 1))
                if b >= 1:
                    pe.wait_ge(a0["exp"], 2 * b)
                for c in range(2):
                    last = pe.matmul(bank[2][:, c * D:c * D + D], thph[b % 2][:, 0, c * P:c * P + P],
                                     thph[b % 2][:, 1, :], start=True, stop=True)
                last.then_inc(a0["sc"], 1)

            def turn_p(b):
                pe.wait_ge(a0["exp"], 2 * (b + 1))
                if b >= 1:
                    pe.wait_ge(a0["pT_sb"], b)
                for j in range(2):
                    for c in range(2):
                        last = pe.transpose(bank[3][:, j * D + c * P:j * D + c * P + P],
                                            p_sb[b % 2][:, c, j * P:j * P + P], ident[:])
                last.then_inc(a0["pT"], 1)

            def weigh(b):
                pe.wait_ge(a0["pT_sb"], b + 1)
                pe.wait_ge(a0["g_sb"], b + 1)
                if b >= 1:
                    pe.wait_ge(a0["txT_sb"], b)
                if b + WEIGH - TURN_X >= 1:
                    pe.wait_ge(norm[1]["lo"], b + WEIGH - TURN_X)
                for c in range(2):
                    for j in range(2):
                        last = pe.matmul(bank[4][:, c * LAT:c * LAT + LAT],
                                         pT_sb[b % 2][:, j * D + c * P:j * D + c * P + P],
                                         g_sb[b % 4][:, j * LAT:j * LAT + LAT], start=j == 0, stop=j == 1)
                last.then_inc(a0["txT"], 1)

            def turn_tx(b):
                pe.wait_ge(a0["txT_sb"], b + 1)
                if b >= 1:
                    pe.wait_ge(a0["tx_sb"], b)
                for c in range(2):
                    last = pe.transpose(bank[5][0:LAT, c * P:c * P + P], txT[b % 2][:, c * LAT:c * LAT + LAT],
                                        ident[:])
                last.then_inc(a0["tx"], 1)

            def means(b):
                if b >= 1:
                    pe.wait_ge(a0["q"], b)
                    pe.wait_ge(a0["mu"], b)
                if b >= 2:
                    pe.wait_ge(a0["var"], b - 1)
                if read := blocks_before(b + MEAN, LOGITS):
                    pe.wait_ge(rout[0]["z"], read)
                if b < NB:
                    pe.wait_ge(a0["ag"], b + 1)
                if b >= 1:
                    last = pe.matmul(bank[6][0:LAT, 1:2], ones[:], q2[:, (b - 1) % 2, :], start=True, stop=True)
                if b < NB:
                    last = pe.matmul(bank[6][0:LAT, 0:1], ones[:], txmv[:, b % 2, 0:1], start=True, stop=True)
                last.then_inc(a0["means"], 1)
                if b == NB - 1:
                    means(NB)

            def lat_out(b):
                pe.wait_ge(a0["h"], b + 1)
                if b >= 1:
                    pe.wait_ge(a0["x"], b)
                pe.matmul(bank[7][:, 0:D], low[:], hr[b % 2], start=True, stop=True).then_inc(a0["w"], 1)

            def rows_bank_free(k):
                pe.wait_ge(a0["txT_sb"], min(k + TURN_X - WEIGH + 1, NB))

            def logits_bank_free(b):
                pe.wait_ge(a0["var"], min(b + LOGITS - MEAN, NB))
                pe.wait_ge(a0["mu"], min(b + LOGITS - MEAN + 1, NB))

            def weights_bank_free(b):
                pe.wait_ge(a0["g_sb"], min(b + TURN_CW - LATENTS + 1, NB))

            pe.wait_ge(small_ok, 16 * N_SMALL)
            pe.wait_ge(const_ok, 3)
            pe.wait_ge(rw_lo_ok, 1)
            run(A_STEPS, (SCORES, scores), (TURN_P, turn_p), (MEAN, means), (WEIGH, weigh), (TURN_TX, turn_tx),
                (TURN_X, turn_rows(1, 4, rows_bank_free)), (LATENTS, latents),
                (TURN_CW, turn_weights(0, 1, weights_bank_free)), (OUT, lat_out), (LOGITS, logits(0, 6, logits_bank_free)))

            def gate_up(layer, n, blk, slot, par, first, tile):
                f = ffn[layer]
                if tile is not None:
                    pe.wait_ge(f["w_lo"], tile + 1)
                x4 = [xT(c, blk * BLK, blk * BLK + BLK) for c in range(DC)]
                if not first:
                    pe.wait_ge(f["silu"], n - 1)
                mm3c(bank[par][:, :], [(w_hi[:, slot, c * P:c * P + P], w_lo[:, slot, c * P:c * P + P])
                                       for c in range(DC)], x4).then_inc(f["g"], 1)
                if not first:
                    pe.wait_ge(f["gu"], n - 1)
                mm3c(bank[2 + par][:, :], [(w_hi[:, slot, (DC + c) * P:(DC + c) * P + P],
                                            w_lo[:, slot, (DC + c) * P:(DC + c) * P + P])
                                           for c in range(DC)], x4).then_inc(f["u"], 1)

            def down(layer, n, slot, par, opens, closes, unit, first):
                f = ffn[layer]
                pe.wait_ge(f["h_lo"], n + 1)
                if opens and not first:
                    pe.wait_ge(f["summed"], unit)
                for c in range(DC):
                    a = WGU + c * P
                    last = mm3(pair_bank[:, c, :], (w_hi[:, slot, a:a + P], w_lo[:, slot, a:a + P]),
                               (h_hi[:, par, :], h_lo[:, par, :]), start=opens, stop=closes)
                last.then_inc(f["down"], 1)

            def experts(layer):
                n_round, left = rounds_of(layer)
                gate_up(layer, 0, 0, 0, 0, True, 0)

                def body(i, first, last):
                    for k in range(4 * NBLK):
                        n = i * 4 * NBLK + k
                        q, m = (k + 1) // (2 * NBLK), (k + 1) % (2 * NBLK)
                        if q < 2:
                            slot = 2 * q + m % 2
                            gate_up(layer, n + 1, m // 2, slot, m % 2, first and k == 0,
                                    i * SLOTS + slot if m < 2 else None)
                        elif not last or left:
                            gate_up(layer, n + 1, 0, 0, 0, False, i * SLOTS + SLOTS)
                        q, m = k // (2 * NBLK), k % (2 * NBLK)
                        down(layer, n, 2 * q + m % 2, k % 2, m % 2 == 0, m % 2 == 1,
                             i * 2 * NBLK + k // 2, first and k == 0)

                body(0, True, False)
                with pe.Fori(1, n_round - 1) as i:
                    body(i, False, False)
                body(n_round - 1, False, True)
                for m in range(left * NBLK):
                    n = n_round * 4 * NBLK + m
                    if m + 1 < left * NBLK:
                        gate_up(layer, n + 1, m + 1, 0, (m + 1) % 2, False, None)
                    down(layer, n, 0, m % 2, True, True, n_round * 2 * NBLK + m, False)
                return n_round * 2 * NBLK + left * NBLK

            units = experts(0)

            def wqkv(j, c, a, b):
                o = (j * DC + c) * D
                return (qkv_hi[:, o + a:o + b], qkv_lo[:, o + a:o + b])

            def sums_to_rows(k):
                pe.wait_ge(ffn[0]["summed"], units)
                if k >= 1:
                    pe.wait_ge(ffn[0]["x"], k)
                if k + B_SUMS - B_TURN >= 1:
                    pe.wait_ge(norm[2]["lo"], k + B_SUMS - B_TURN)
                turn_sums(0, k, 6)

            def project(b):
                B, j = b // PER, b % PER
                pe.wait_ge(norm[2]["lo"], PER * B + PER)
                if b >= 2:
                    pe.wait_ge(a1["proj_sb"], b - 1)
                a = j % DC * P
                mm3c(bank[j % 2][:, :], [wqkv(j // DC, c, a, a + P) for c in range(DC)],
                     [xT(c, B * BLK, B * BLK + BLK) for c in range(DC)]).then_inc(a1["proj"], 1)

            def values(b):
                if b >= 1:
                    pe.wait_ge(a1["v_sb"], b)
                mm3c(bank[2][:, 0:D], [xT(c, b * P, b * P + P) for c in range(DC)],
                     [wqkv(2, c, 0, D) for c in range(DC)]).then_inc(a1["v"], 1)

            def scores1(b):
                B, o = b // PER, b % PER * P
                pe.wait_ge(a1["proj_sb"], PER * (B + 1))
                if b >= 1:
                    pe.wait_ge(a1["sm"], b)
                for c in range(DC):
                    last = pe.matmul(bank[3][:, 0:P], QT[B % 2][:, c, o:o + P], KT[B % 2][:, c, o:o + P],
                                     start=c == 0, stop=c == DC - 1)
                last.then_inc(a1["sc"], 1)

            def turn_p1(b):
                step = b + B_TURN_P
                pe.wait_ge(a1["exp"], b + 1)
                if b >= 1:
                    pe.wait_ge(a1["pT_sb"], b)
                if read := blocks_before(step, B_LOGITS):
                    pe.wait_ge(rout[1]["z"], read)
                if turned := blocks_before(step, B_TURN_CW):
                    pe.wait_ge(rout[1]["turned"], turned)
                pe.transpose(bank[4][:, 0:P], pr[b % 2], ident[:]).then_inc(a1["pT"], 1)

            def weigh1(b):
                pe.wait_ge(a1["pT_sb"], b + 1)
                pe.wait_ge(a1["v_sb"], b + 1)
                if b >= 1:
                    pe.wait_ge(a1["x"], b)
                pe.matmul(bank[5][:, 0:D], prT[b % 2], V_sb[b % 4], start=True, stop=True).then_inc(a1["o"], 1)

            def logits1_bank_free(b):
                step = b + B_LOGITS
                pe.wait_ge(a1["pT_sb"], min(step - B_TURN_P + 1, NB))
                if turned := blocks_before(step, B_TURN_CW):
                    pe.wait_ge(rout[1]["turned"], turned)

            def weights1_bank_free(b):
                step = b + B_TURN_CW
                pe.wait_ge(a1["pT_sb"], min(step - B_TURN_P + 1, NB))
                pe.wait_ge(rout[1]["z"], blocks_before(step, B_LOGITS))

            pe.wait_ge(qkv_lo_ok, 1)
            run(B_STEPS, (B_SUMS, sums_to_rows), (B_SCORES, scores1), (B_TURN_P, turn_p1),
                (B_PROJ + PER - 1, project), (B_SCORES, values), (B_OUT, weigh1),
                (B_TURN, turn_rows(2, 6, lambda k: pe.wait_ge(ffn[0]["x"], min(k + B_TURN - B_SUMS + 1, NB)))),
                (B_TURN3, turn_rows(3, 7, lambda k: None)),
                (B_LOGITS, logits(1, 4, logits1_bank_free)), (B_TURN_CW, turn_weights(1, 4, weights1_bank_free)))

            units = experts(1)
            pe.wait_ge(ffn[1]["summed"], units)
            for k in range(NB):
                if k >= 2:
                    pe.wait_ge(ffn[1]["x"], k - 1)
                turn_sums(1, k, 4 + k % 2)


def _tiles(gate, up, down, np):
    n = gate.shape[0] // P

    def turned(w):
        return w.reshape(n, P, DC, P).transpose(0, 3, 2, 1).reshape(n, P, DC * P)

    return np.ascontiguousarray(np.concatenate([turned(gate), turned(up), down.reshape(n, P, D)], axis=2))


def kernel(**inputs):
    import numpy as np
    import concourse.bacc as _bacc
    from concourse import mybir as _mybir
    from concourse.bass_utils import run_bass_kernel_spmd as _run

    a = {k: np.asarray(v) for k, v in inputs.items()}
    c = np.ascontiguousarray

    def wide(v):
        return c(np.broadcast_to(v.reshape(1, -1), (P, v.size)))

    def chunks(w):
        return w.T.reshape(DC, P, -1).transpose(1, 0, 2)

    def router_cols(w):
        return np.concatenate([w, np.zeros((NL - w.shape[0], D), w.dtype)])

    g0 = np.concatenate([a["L0_ffn_Wg"].transpose(0, 2, 1).reshape(-1, D), a["L0_ffn_sWg"].T])
    u0 = np.concatenate([a["L0_ffn_Wu"].transpose(0, 2, 1).reshape(-1, D), a["L0_ffn_sWu"].T])
    d0 = np.concatenate([a["L0_ffn_Wd"].reshape(-1, D), a["L0_ffn_sWd"]])
    egu, sgu = a["L1_ffn_expert_gate_up"], a["L1_ffn_shared_gate_up"]
    I, SI = egu.shape[1] // 2, sgu.shape[0] // 2
    pad = np.zeros((TILES[1] * P - NE * I - SI, D), egu.dtype)
    g1 = np.concatenate([egu[:, :I].reshape(-1, D), sgu[:SI], pad])
    u1 = np.concatenate([egu[:, I:].reshape(-1, D), sgu[SI:], pad])
    d1 = np.concatenate([a["L1_ffn_expert_down"].transpose(0, 2, 1).reshape(-1, D), a["L1_ffn_shared_down"].T, pad])
    arrays = {
        "x_in": c(a["x"]),
        "ctx_in": c(a["ctx_2048"]),
        "mask_in": c(a["mask_BxSxS2_ff0"]),
        "gates_in": wide(np.concatenate([a["g_xattn"], a["g_ffn"]])),
        "ident_in": np.eye(P, dtype=np.float32),
        "lat_w": c(np.stack([a["L0_xattn_theta_w"].T, a["L0_xattn_phi_w"].T, a["L0_xattn_g_w"].T], axis=1)),
        "lat_b": c(np.stack([a["L0_xattn_theta_b"], a["L0_xattn_phi_b"], a["L0_xattn_g_b"]], axis=1)),
        "lat_out_w": c(a["L0_xattn_out_w"].T),
        "lat_out_b": c(a["L0_xattn_out_b"].reshape(P, 1)),
        "lat_norm": c(np.stack([a["L0_xattn_ln_gamma"], a["L0_xattn_ln_beta"]], axis=1)),
        "qkv_w": c(np.stack([chunks(a[f"L1_xattn_W{n}"]) for n in "qkv"], axis=1).reshape(P, -1)),
        "qk_b": c(np.stack([a[f"L1_xattn_b{n}"].reshape(DC, P).T for n in "qk"], axis=1)),
        "v_b": wide(a["L1_xattn_bv"]),
        "router_w": c(np.stack([chunks(router_cols(a["L0_ffn_Wr"])).reshape(P, -1),
                                chunks(router_cols(np.concatenate([a["L1_ffn_gate_w"],
                                                                   a["L1_ffn_shared_gate_vec"]]))).reshape(P, -1)],
                               axis=1)),
        "router_b": wide(a["L0_ffn_bias"]),
        "ffn_w0": _tiles(g0, u0, d0, np),
        "ffn_w1": _tiles(g1, u1, d1, np),
    }
    nc = _bacc.Bacc("TRN2", target_bir_lowering=False, num_devices=1)
    ap = {n: nc.dram_tensor(n, v.shape, _mybir.dt.from_np(v.dtype), kind="ExternalInput").ap()
          for n, v in arrays.items()}
    out = nc.dram_tensor("out", (NB, P, D), _mybir.dt.float32, kind="ExternalOutput").ap()
    tiles = [ap.pop("ffn_w0"), ap.pop("ffn_w1")]
    gated_blocks(nc, out=out, ffn_w=tiles, **ap)
    r = _run(nc, [arrays], core_ids=[0])
    return r.results[0]["out"]
```

```python
from contextlib import ExitStack

import concourse.bass as bass
from concourse import mybir

F32 = mybir.dt.float32
F32R = mybir.dt.float32r
ALU = mybir.AluOpType
ACT = mybir.ActivationFunctionType
AX_X = mybir.AxisListType.X

P = 128
NB, D = 16, 256
DC = D // P
LAT = 64
BLK = 512
NBLK = NB * P // BLK
PER = BLK // P
NE = 16
NCW = NE + 1
NL = NCW + 1
NSENT = 8
GRAIN = 16
WGU, WD = 2 * DC * P, D
WT = WGU + WD
TILES = (17, 28)
TOPK = (2, 4)
TOPK_EPS = 1e-9
LN_EPS = 1e-5
EXPERT = (P, 176)
SLOTS = 4


def gated_blocks(nc, x_in, ctx_in, mask_in, gates_in, ident_in,
                 lat_w, lat_b, lat_out_w, lat_out_b, lat_norm,
                 qkv_w, qk_b, v_b, router_w, router_b, ffn_w, out):
    with ExitStack() as ctx:
        def sb(name, shape, dt=F32):
            return ctx.enter_context(nc.sbuf_tensor(name, shape, dt))

        def sem(name):
            return ctx.enter_context(nc.semaphore(name))

        x = sb("x", [P, NB, D])
        xn_comb = sb("xn_comb", [P, NB * D])
        xn = xn_comb[:, :].rearrange("p (b d) -> p b d", b=NB)
        comb = xn_comb[:, :].rearrange("p (b j n) -> p b j n", b=NBLK, j=2)
        xT_hi = sb("xT_hi", [P, DC, NB * P], F32R)
        xT_lo = sb("xT_lo", [P, DC, NB * P], F32R)
        ctx_accT = sb("ctx_accT", [P, NB * D])
        ctx_sb = ctx_accT[:, :].rearrange("p (b d) -> p b d", b=NB)
        accT = ctx_accT[:, :].rearrange("p (c n) -> p c n", c=DC)
        mask = sb("mask", [P, NB, P])
        ident = sb("ident", [P, P])
        tg = sb("tg", [P, 4])
        mhalf = sb("mhalf", [P, NB])
        ones = sb("ones", [LAT, LAT])
        bn6 = sb("bn6", [P, NB, 6])
        mv = sb("mv", [P, NB, 2])
        ve = sb("ve", [P, NB])
        rstd = sb("rstd", [P, NB])
        lw = sb("lw", [P, 3, LAT])
        lb = sb("lb", [LAT, 3])
        low = sb("low", [LAT, P])
        lob = sb("lob", [P, 1])
        lnorm = sb("lnorm", [LAT, 2, D])
        shared_bufs = sb("shared_bufs", [P, 6656])
        at = [0]

        def part(n, rows=P):
            a = at[0]
            at[0] += n
            return shared_bufs[0:rows, a:a + n]

        thph = [part(2 * D, LAT).rearrange("p (a t) -> p a t", a=2) for _ in range(2)]
        g_sb = [part(2 * LAT) for _ in range(4)]
        txT = [part(2 * LAT) for _ in range(2)]
        p_sb = [part(2 * D).rearrange("p (c s) -> p c s", c=2) for _ in range(2)]
        pT_sb = [part(2 * D) for _ in range(2)]
        tx = [part(D, LAT) for _ in range(4)]
        hu = [part(D, LAT) for _ in range(2)]
        hv = [part(D, LAT) for _ in range(2)]
        hr = [part(D, LAT) for _ in range(2)]
        assert at[0] <= 6656
        at[0] = 0
        QT = [part(DC * BLK).rearrange("p (c n) -> p c n", c=DC) for _ in range(2)]
        KT = [part(DC * BLK).rearrange("p (c n) -> p c n", c=DC) for _ in range(2)]
        V_sb = [part(D) for _ in range(4)]
        sm = [part(P) for _ in range(2)]
        pr = [part(P) for _ in range(2)]
        prT = [part(P) for _ in range(2)]
        assert at[0] <= 6656
        nmx = sb("nmx", [P, 2, 2])
        rs = sb("rs", [P, 4, 2])
        rr = sb("rr", [P, 2, 2])
        tx6 = sb("tx6", [LAT, 2, 6])
        txmv = sb("txmv", [LAT, 2, 2])
        mu = sb("mu", [LAT, 4, 1])
        dmu = sb("dmu", [LAT, 2, 1])
        q2 = sb("q2", [LAT, 2, 1])
        hve = sb("hve", [LAT, 2, 1])
        hrstd = sb("hrstd", [LAT, 2, 1])
        qkv_raw = sb("qkv_raw", [P, 3 * DC * D])
        qkv_hi = sb("qkv_hi", [P, 3 * DC * D], F32R)
        qkv_lo = sb("qkv_lo", [P, 3 * DC * D], F32R)
        qkb = sb("qkb", [P, 2, DC])
        vb = sb("vb", [P, D])
        nmx1 = sb("nmx1", [P, 2, 1])
        rs1 = sb("rs1", [P, 4, 1])
        rr1 = sb("rr1", [P, 2, 1])
        rt1 = sb("rt1", [P, 2, 1])
        rw_raw = sb("rw_raw", [P, 2, DC * NL])
        rw = sb("rw", [P, 2 * DC, 2, NL], F32R)
        rb = sb("rb", [P, NE])
        z = sb("z", [P, PER, NCW])
        ez = sb("ez", [P, PER, NE])
        es = sb("es", [P, PER])
        rowst = sb("rowst", [P, PER])
        rowrc = sb("rowrc", [P, PER])
        probs = sb("probs", [P, PER, NE + NSENT])
        rest = sb("rest", [P, PER, NE + NSENT])
        top8 = sb("top8", [P, PER, 8])
        cw = sb("cw", [P, PER, NCW])
        cwT = sb("cwT", [NCW, 2, BLK])
        cw_rows = [nc.dram_tensor("cw_rows0", (NCW, NB * P), F32, kind="Internal").ap(),
                   nc.dram_tensor("cw_rows1", (TILES[1] * P // GRAIN, NB * P), F32, kind="Internal").ap()]
        w_raw = sb("w_raw", [P, SLOTS, WT])
        w_hi = sb("w_hi", [P, SLOTS, WT], F32R)
        w_lo = sb("w_lo", [P, SLOTS, WT], F32R)
        sg = sb("sg", [P, 2, BLK])
        gu = sb("gu", [P, BLK])
        hh = sb("hh", [P, 2, BLK])
        h_hi = sb("h_hi", [P, 2, BLK], F32R)
        h_lo = sb("h_lo", [P, 2, BLK], F32R)

        bank = [ctx.enter_context(nc.psum_tensor(f"bank{i}", [P, BLK], F32)) for i in range(6)]
        pair_bank = ctx.enter_context(nc.psum_tensor("pair_bank", [P, DC, BLK], F32))
        bank += [pair_bank[:, c, :] for c in range(DC)]

        x_in_ok = [sem(f"x_in_ok{g}") for g in range(NBLK)]
        small_ok, later_ok, out_ok = sem("small_ok"), sem("later_ok"), sem("out_ok")
        ctx_ok = [sem(f"ctx_ok{g}") for g in range(NBLK)]
        tanh_ok, const_ok, rw_hi_ok, rw_lo_ok = sem("tanh_ok"), sem("const_ok"), sem("rw_hi_ok"), sem("rw_lo_ok")
        qkv_hi_ok, qkv_lo_ok = sem("qkv_hi_ok"), sem("qkv_lo_ok")
        N_SMALL = 9

        names = ("stats", "aggr", "var", "rstd", "xn", "xTp", "hi", "lo")
        norm = [dict(zip(names, (sem(f"norm{n}_{s}") for s in names))) for n in range(4)]
        names = ("logits", "z", "centred", "exp", "step", "cw", "cwT", "turned", "stored")
        rout = [dict(zip(names, (sem(f"router{n}_{s}") for s in names))) for n in range(2)]
        names = ("w_hi", "w_lo", "g", "u", "silu", "gu", "h", "h_hi", "h_lo", "down", "summed",
                 "turned", "x")
        ffn = [dict(zip(names, (sem(f"ffn{n}_{s}") for s in names))) for n in range(2)]
        raw_ok = [[sem(f"raw{n}_ok{s}") for s in range(SLOTS)] for n in range(2)]
        comb_ok = [[sem(f"comb{n}_ok{b}") for b in range(NBLK)] for n in range(2)]
        names = ("thph", "thph_sb", "g_sb", "sc", "max", "exp", "rec", "pT", "pT_sb", "txT", "txT_sb", "tx",
                 "tx_sb", "st", "ag", "means", "mu", "d", "q", "var", "rstd", "u", "v", "h", "w", "ctx", "res", "x")
        a0 = dict(zip(names, (sem(f"lat_{s}") for s in names)))
        names = ("vb", "proj", "proj_sb", "v", "v_sb", "sc", "sm", "max", "exp", "rec", "rt", "pT", "pT_sb", "o",
                 "res", "x")
        a1 = dict(zip(names, (sem(f"att_{s}") for s in names)))

        block = ctx.enter_context(nc.Block())

        def rounds_of(layer):
            n = TILES[layer] // SLOTS
            assert TILES[layer] - SLOTS * n <= 1
            return (n, TILES[layer] - SLOTS * n)

        def pair_done(round_, slot):
            return (round_ * 2 + slot // 2 - 1) * 2 * NBLK

        def run(steps, *stages):
            for i in range(steps):
                for lag, stage in stages:
                    if 0 <= i - lag < NB:
                        stage(i - lag)

        def two(stage):
            def both(i):
                for b in range(2 * i, min(2 * i + 2, NB)):
                    stage(b)
            return both

        def last_of_block(b):
            return b % PER == PER - 1

        FIRST = SLOTS * NBLK

        def final_batches(k):
            a = 2 * (k - FIRST + 2 * NBLK - 2)
            if k == FIRST:
                return list(range(a, NB))
            return list(range(a, a + 2)) if a >= 0 else []

        def first_round(k):
            return k // SLOTS, k % SLOTS, k % SLOTS < 2

        A_STEPS = NB + 14
        A_SPLIT, A_FFN = 8, 19
        LOAD, NORM, LATENTS, SCORES, TURN_P, WEIGH, TURN_TX, MEAN, VAR, OUT = 0, 1, 2, 3, 4, 5, 6, 7, 8, 9
        STATS, XN, TURN_X, LOGITS, TURN_CW = 9, 10, 11, 12, 14
        B_STEPS = NB + 15
        B_SPLIT, B_FFN = 12, 20
        B_SUMS, B_XN, B_TURN, B_PROJ, B_SCORES, B_TURN_P, B_OUT = 0, 1, 2, 4, 8, 9, 10
        B_XN3, B_TURN3, B_LOGITS, B_TURN_CW = 11, 12, 13, 15
        EARLY = A_STEPS - A_FFN
        assert EARLY == B_STEPS - B_FFN and EARLY % 2 == 1
        QKV_STEPS = range(EARLY, EARLY + 3)

        A_THPH, A_G, A_SCORES, A_P, A_TX, A_TURNTX, A_MEANS, A_OUT = 0, 2, 6, 7, 1, 3, 4, 5
        B_SUM, B_ROWS, B_PROJECT, B_V, B_SC, B_P, B_O = 0, 2, 6, 1, 3, 4, 5
        LOGITS_BANK, CW_BANK = (A_MEANS, B_P), (A_TURNTX, B_V)

        def rows3_bank(k):
            return B_PROJECT + 1 if k + B_TURN3 < B_FFN else B_O

        def ffn_bank(n, par):
            return 0 if isinstance(n, int) and n < EARLY else par

        @block.sync
        def _(sp):
            for g in range(NBLK):
                sp.dma_start(x[:, PER * g:PER * g + PER, :],
                             x_in[PER * g:PER * g + PER].rearrange("b p d -> p b d")).then_inc(x_in_ok[g], 16)
                if g == 0:
                    small = [(gates_in, tg), (ident_in, ident), (lat_w, lw), (lat_b, lb), (lat_out_w, low),
                             (lat_out_b, lob), (lat_norm, lnorm), (router_w, rw_raw), (router_b, rb)]
                    assert len(small) == N_SMALL
                    for src, dst in small:
                        sp.dma_start(dst[:], src).then_inc(small_ok, 16)
                sp.dma_start(ctx_sb[:, PER * g:PER * g + PER, :],
                             ctx_in[PER * g:PER * g + PER].rearrange("b p d -> p b d")).then_inc(ctx_ok[g], 16)

            def load_tile(layer, t, slot):
                if not (isinstance(t, int) and t < SLOTS):
                    sp.wait_ge(ffn[layer]["w_lo"], t - SLOTS + 1)
                elif layer == 1:
                    sp.wait_ge(ffn[0]["w_lo"], TILES[0])
                sp.dma_start(w_raw[:, slot, :], ffn_w[layer][t]).then_inc(raw_ok[layer][slot], 16)

            def load_comb(layer, t, blk, j):
                cols = slice(blk * BLK, blk * BLK + BLK)
                if layer == 0:
                    src = cw_rows[0][t, cols].unsqueeze(0).to_broadcast([P, BLK])
                    sp.dma_start(comb[:, blk, j, :], src).then_inc(comb_ok[0][blk], 16)
                else:
                    src = cw_rows[1].rearrange("(t g) n -> t g n", g=P // GRAIN)[t][:, cols]
                    sp.dma_start(comb[:, blk, j, :],
                                 src.unsqueeze(1).to_broadcast([P // GRAIN, GRAIN, BLK]))\
                        .then_inc(comb_ok[1][blk], 16)

            def store_weights(layer, g):
                s = rout[layer]
                sp.wait_ge(s["turned"], g + 1)
                cols = slice(g * BLK, g * BLK + BLK)
                if layer == 0:
                    sp.dma_start(cw_rows[0][:, cols], cwT[:, g % 2, :]).then_inc(s["stored"], 16)
                    stored = 16
                else:
                    n = EXPERT[1] // GRAIN
                    sp.dma_start(cw_rows[1][0:NE * n, cols].rearrange("(e r) n -> e r n", r=n),
                                 cwT[0:NE, g % 2, :].unsqueeze(1).to_broadcast([NE, n, BLK]))\
                        .then_inc(s["stored"], 16)
                    n = TILES[1] * P // GRAIN - NE * n
                    sp.dma_start(cw_rows[1][NE * EXPERT[1] // GRAIN:, cols].unsqueeze(0),
                                 cwT[NE:NCW, g % 2, :].unsqueeze(1).to_broadcast([1, n, BLK]))\
                        .then_inc(s["stored"], 16)
                    stored = 32
                sp.wait_ge(s["stored"], stored * (g + 1))
                sp.wait_ge(norm[1 + 2 * layer]["lo"], PER * g + PER)
                for j in range(2):
                    load_comb(layer, j, g, j)

            def load_later():
                for src, dst in [(qkv_w, qkv_raw[:]), (qk_b, qkb[:]), (v_b, vb[:]),
                                 (mask_in.rearrange("b p k -> p b k"), mask[:])]:
                    sp.dma_start(dst, src).then_inc(later_ok, 16)

            for layer in range(2):
                f = ffn[layer]
                for t in range(SLOTS):
                    load_tile(layer, t, t)
                if layer == 0:
                    load_later()
                for t in range(SLOTS):
                    load_tile(layer, SLOTS + t, t)

                store_weights(layer, 0)
                for u in range(2 * NBLK):
                    sp.wait_ge(f["h"], 2 * u + 2)
                    for j in range(2):
                        load_comb(layer, 2 + u % 2 * 2 + j, u // 2, j)
                    if u % 2 == 0 and u // 2 + 1 < NBLK:
                        store_weights(layer, u // 2 + 1)
                n_round, left = rounds_of(layer)

                def body(i, last):
                    for q in range(2):
                        for b in range(NBLK):
                            more = 2 if not last or q == 0 else left
                            if b == 0 and not last:
                                for j in range(2):
                                    load_tile(layer, i * SLOTS + SLOTS + 2 * q + j, 2 * q + j)
                            elif b == 0 and q == 0 and left:
                                load_tile(layer, n_round * SLOTS, 0)
                            if more:
                                sp.wait_ge(f["h"], i * 4 * NBLK + (q * NBLK + b) * 2 + 2)
                            for j in range(more):
                                load_comb(layer, i * SLOTS + 2 * q + 2 + j, b, j)

                with sp.Fori(1, n_round - 1) as i:
                    body(i, False)
                body(n_round - 1, True)
            for k in range(NB):
                sp.wait_ge(ffn[1]["x"], k + 1)
                sp.dma_start(out[k], x[:, k, :]).then_inc(out_ok, 16)
            sp.wait_ge(out_ok, 16 * NB)

        @block.gpsimd
        def _(pool):
            pool.memset(mhalf[:], -0.5).then_inc(const_ok, 1)
            pool.memset(ones[:], 1.0 / LAT).then_inc(const_ok, 1)
            pool.memset(probs[:], -1.0).then_inc(const_ok, 1)
            pool.wait_ge(const_ok, 3)
            pool.wait_ge(small_ok, 16 * N_SMALL)
            pool.wait_ge(tanh_ok, 1)

            def row_rstd(n):
                def stage(b):
                    pool.wait_ge(norm[n]["var"], b + 1)
                    pool.tensor_tensor(rstd[:, b:b + 1], ve[:, b:b + 1], mhalf[:, 0:1], ALU.pow)\
                        .then_inc(norm[n]["rstd"], 1)
                return stage

            def add_context(b):
                pool.wait_ge(norm[0]["xn"], b + 1)
                pool.wait_ge(ctx_ok[b // PER], 16)
                pool.wait_ge(a0["thph"], b + 1)
                pool.tensor_scalar(ctx_sb[:, b, :], ctx_sb[:, b, :], lob[:, 0:1], tg[:, 0:1], ALU.add, ALU.mult)\
                    .then_inc(a0["ctx"], 1)
                pool.wait_ge(a0["ctx"], b + 1)
                pool.tensor_tensor(x[:, b, :], x[:, b, :], ctx_sb[:, b, :], ALU.add).then_inc(a0["res"], 1)

            def lat_rstd(b):
                pool.wait_ge(a0["var"], b + 1)
                pool.tensor_tensor(hrstd[:, b % 2, :], hve[:, b % 2, :], mhalf[0:LAT, 0:1], ALU.pow)\
                    .then_inc(a0["rstd"], 1)

            run(A_STEPS,
                (VAR, lat_rstd), (STATS, row_rstd(1)), (LATENTS, add_context), (LOAD, two(row_rstd(0))))
            pool.wait_ge(later_ok, 16 * 4)
            pool.tensor_scalar(vb[:], vb[:], tg[:, 1:2], None, ALU.mult).then_inc(a1["vb"], 1)
            pool.wait_ge(a1["vb"], 1)

            def add_v_bias(b):
                pool.wait_ge(norm[2]["xn"], b + 1)
                pool.tensor_tensor(x[:, b, :], x[:, b, :], vb[:], ALU.add).then_inc(a1["res"], 1)

            run(B_STEPS,
                (B_SUMS, two(row_rstd(2))), (B_XN, two(add_v_bias)), (B_OUT, row_rstd(3)))

        @block.scalar
        def _(act):
            act.wait_ge(small_ok, 16 * N_SMALL)
            act.activation(tg[:], tg[:], ACT.Tanh).then_inc(tanh_ok, 1)
            act.activation(rw[:, :, 0, :], rw_raw[:].rearrange("p l (c n) -> p (l c) n", c=DC),
                           ACT.Copy).then_inc(rw_hi_ok, 1)

            def split_rows(n, src):
                def stage(k):
                    act.wait_ge(norm[n]["xTp"], k + 1)
                    act.activation(xT_hi[:, :, k * P:k * P + P],
                                   bank[src(k)][:, 0:D].rearrange("p (c n) -> p c n", c=DC),
                                   ACT.Copy).then_inc(norm[n]["hi"], 1)
                return stage

            def split_pair(n, src):
                def stage(i):
                    if 2 * i < NB:
                        act.wait_ge(norm[n]["xTp"], 2 * i + 2)
                        act.activation(xT_hi[:, :, 2 * i * P:2 * i * P + 2 * P],
                                       bank[src][:, :].rearrange("p (c n) -> p c n", c=DC),
                                       ACT.Copy).then_inc(norm[n]["hi"], 2)
                return stage

            def router_exp(layer):
                def stage(b):
                    if last_of_block(b):
                        g, s = b // PER, rout[layer]
                        act.wait_ge(s["centred"], g + 1)
                        act.activation(ez[:], z[:, :, 0:NE], ACT.Exp).then_inc(s["exp"], 1)
                        if layer == 1:
                            act.activation(es[:], z[:, :, NE], ACT.Exp, scale=-1.0).then_inc(s["exp"], 1)
                return stage

            def router_out(layer):
                def stage(b):
                    if last_of_block(b):
                        g, s = b // PER, rout[layer]
                        act.wait_ge(s["cwT"], g + 1)
                        if g >= 2:
                            act.wait_ge(s["stored"], (16, 32)[layer] * (g - 1))
                        act.activation(cwT[:, g % 2, :], bank[CW_BANK[layer]][0:NCW, :], ACT.Copy)\
                            .then_inc(s["turned"], 1)
                return stage

            def split_tile(layer, slot, round_, downs):
                f = ffn[layer]
                act.wait_ge(raw_ok[layer][slot], 16 * (round_ + 1))
                if downs is not None:
                    act.wait_ge(f["down"], downs)
                elif layer == 1:
                    act.wait_ge(ffn[0]["down"], TILES[0] * NBLK)
                act.activation(w_hi[:, slot, :], w_raw[:, slot, :], ACT.Copy).then_inc(f["w_hi"], 1)

            def silu(layer, n, par, first):
                f = ffn[layer]
                act.wait_ge(f["g"], n + 1)
                if not first:
                    act.wait_ge(f["gu"], n - 1)
                act.activation(sg[:, par, :], bank[ffn_bank(n, par)][:, :], ACT.Silu).then_inc(f["silu"], 1)

            def hidden_high(layer, n, par, first):
                f = ffn[layer]
                act.wait_ge(f["h"], n + 1)
                if not first:
                    act.wait_ge(f["down"], n - 1)
                act.activation(h_hi[:, par, :], hh[:, par, :], ACT.Copy).then_inc(f["h_hi"], 1)

            def early_split(layer):
                def stage(t):
                    if t < SLOTS:
                        split_tile(layer, t, 0, None)
                return stage

            def hidden(layer, n, par):
                silu(layer, n, par, False)
                hidden_high(layer, n, par, False)

            def early(part, layer):
                def stage(k):
                    if k < EARLY - 1:
                        part(layer, k, k % 2, k < 2)
                return stage

            def latents_out(b):
                act.wait_ge(a0["thph"], b + 1)
                if b >= 2:
                    act.wait_ge(a0["sc"], b - 1)
                for j in range(2):
                    act.activation(thph[b % 2][:, j, :], bank[A_THPH][0:LAT, j * D:j * D + D], ACT.Identity,
                                   bias=lb[:, j:j + 1]).then_inc(a0["thph_sb"], 1)
                if b >= 4:
                    act.wait_ge(a0["txT"], b - 3)
                act.activation(g_sb[b % 4], bank[A_G][:, 0:2 * LAT], ACT.Copy).then_inc(a0["g_sb"], 1)

            def exps(b):
                act.wait_ge(a0["max"], b + 1)
                if b >= 2:
                    act.wait_ge(a0["pT"], b - 1)
                if b >= 4:
                    act.wait_ge(a0["rec"], b - 3)
                for c in range(2):
                    act.activation(p_sb[b % 2][:, c, :], bank[A_SCORES][:, c * D:c * D + D], ACT.Exp,
                                   bias=nmx[:, b % 2, c:c + 1], accum_out=rs[:, b % 4, c:c + 1])\
                        .then_inc(a0["exp"], 1)

            def pT_out(b):
                act.wait_ge(a0["pT"], b + 1)
                if b >= 2:
                    act.wait_ge(a0["txT"], b - 1)
                act.activation(pT_sb[b % 2], bank[A_P][:, :], ACT.Copy).then_inc(a0["pT_sb"], 1)

            def tx_out(b):
                act.wait_ge(a0["tx"], b + 1)
                if b >= 4:
                    act.wait_ge(a0["u"], b - 3)
                act.activation(tx[b % 4], bank[A_TURNTX][0:LAT, 0:D], ACT.Identity, bias=lb[:, 2:3])\
                    .then_inc(a0["tx_sb"], 1)

            def relu(b):
                act.wait_ge(a0["v"], b + 1)
                if b >= 2:
                    act.wait_ge(a0["w"], b - 1)
                act.activation(hr[b % 2], hv[b % 2], ACT.Relu).then_inc(a0["h"], 1)

            run(A_STEPS,
                (TURN_P, pT_out), (SCORES, exps), (TURN_TX, tx_out), (A_FFN + 1, early(silu, 0)),
                (TURN_X, split_rows(1, lambda k: A_TX)), (LATENTS, latents_out), (VAR, relu),
                (LOGITS, router_exp(0)), (TURN_CW, router_out(0)), (A_SPLIT, early_split(0)),
                (A_FFN + 1, early(hidden_high, 0)))

            def experts(layer):
                n_round, left = rounds_of(layer)

                for k in range(EARLY - 1, FIRST):
                    hidden(layer, k, k % 2)
                    if layer == 0 and k in QKV_STEPS:
                        a = QKV_STEPS.index(k) * DC * D
                        act.wait_ge(later_ok, 16 * 4)
                        act.activation(qkv_hi[:, a:a + DC * D], qkv_raw[:, a:a + DC * D], ACT.Copy)\
                            .then_inc(qkv_hi_ok, 1)
                    if k >= FIRST - 2:
                        split_tile(layer, k % 2, 1, FIRST - 2)

                def body(i, last):
                    for q in range(2):
                        for m in range(2 * NBLK):
                            hidden(layer, i * FIRST + q * 2 * NBLK + m, m % 2)
                            if m in (3, 5):
                                slot = (2 * q + 2 + (m == 5)) % SLOTS
                                r = i if q == 0 else i + 1
                                if q == 0 or not last or slot < left:
                                    split_tile(layer, slot, r, pair_done(r, slot))

                with act.Fori(1, n_round - 1) as i:
                    body(i, False)
                body(n_round - 1, True)
                for m in range(left * NBLK):
                    hidden(layer, n_round * 4 * NBLK + m, m % 2)

            experts(0)


            def proj_out(b):
                B, j = b // PER, b % PER
                act.wait_ge(a1["proj"], b + 1)
                if B >= 2:
                    act.wait_ge(a1["sc"], PER * (B - 1))
                act.activation((QT, KT)[j // DC][B % 2][:, j % DC, :], bank[B_PROJECT][:, :], ACT.Identity,
                               bias=qkb[:, j // DC, j % DC:j % DC + 1]).then_inc(a1["proj_sb"], 1)

            def v_out(b):
                act.wait_ge(a1["v"], b + 1)
                if b >= 4:
                    act.wait_ge(a1["o"], b - 3)
                act.activation(V_sb[b % 4], bank[B_V][:, 0:D], ACT.Copy).then_inc(a1["v_sb"], 1)

            def exp1(b):
                act.wait_ge(a1["max"], b + 1)
                if b >= 2:
                    act.wait_ge(a1["pT"], b - 1)
                if b >= 4:
                    act.wait_ge(a1["rec"], b - 3)
                act.activation(pr[b % 2], sm[b % 2], ACT.Exp, bias=nmx1[:, b % 2, :],
                               accum_out=rs1[:, b % 4, :]).then_inc(a1["exp"], 1)

            def prT_out(b):
                act.wait_ge(a1["pT"], b + 1)
                if b >= 2:
                    act.wait_ge(a1["o"], b - 1)
                act.activation(prT[b % 2], bank[B_P][:, 0:P], ACT.Copy).then_inc(a1["pT_sb"], 1)

            run(B_STEPS,
                (B_FFN + 1, early(silu, 1)), (B_TURN_P, prT_out), (B_SCORES, exp1),
                (B_TURN, split_pair(2, B_ROWS)), (B_PROJ, proj_out), (B_SCORES, v_out),
                (B_TURN3, split_rows(3, rows3_bank)), (B_LOGITS, router_exp(1)), (B_TURN_CW, router_out(1)),
                (B_SPLIT, early_split(1)), (B_FFN + 1, early(hidden_high, 1)))
            experts(1)

        @block.vector
        def _(dve):
            dve.wait_ge(small_ok, 16 * N_SMALL)
            dve.wait_ge(rw_hi_ok, 1)
            dve.tensor_tensor(rw[:, :, 1, :], rw_raw[:].rearrange("p l (c n) -> p (l c) n", c=DC),
                              rw[:, :, 0, :].bitcast(F32), ALU.subtract).then_inc(rw_lo_ok, 1)
            dve.wait_ge(tanh_ok, 1)
            dve.wait_ge(const_ok, 3)

            def row_stats(n, ready):
                def stage(b):
                    s = norm[n]
                    ready(b)
                    dve.bn_stats(bn6[:, b, :], x[:, b, :]).then_inc(s["stats"], 1)
                return stage

            def row_aggregate(n):
                def stage(b):
                    s = norm[n]
                    dve.wait_ge(s["stats"], b + 1)
                    dve.bn_aggr(mv[:, b, :], bn6[:, b, :]).then_inc(s["aggr"], 1)
                return stage

            def normalise(n):
                def stage(b):
                    s = norm[n]
                    dve.wait_ge(s["rstd"], b + 1)
                    dve.tensor_scalar(xn[:, b, :], x[:, b, :], mv[:, b, 0:1], rstd[:, b:b + 1],
                                      ALU.subtract, ALU.mult).then_inc(s["xn"], 1)
                return stage

            def split_rows(n, src):
                def stage(k):
                    dve.wait_ge(norm[n]["hi"], k + 1)
                    dst = slice(k * P, k * P + P)
                    dve.tensor_tensor(xT_lo[:, :, dst], bank[src(k)][:, 0:D].rearrange("p (c n) -> p c n", c=DC),
                                      xT_hi[:, :, dst].bitcast(F32), ALU.subtract).then_inc(norm[n]["lo"], 1)
                return stage

            def split_pair(n, src):
                def stage(i):
                    if 2 * i < NB:
                        dve.wait_ge(norm[n]["hi"], 2 * i + 2)
                        dst = slice(2 * i * P, 2 * i * P + 2 * P)
                        dve.tensor_tensor(xT_lo[:, :, dst], bank[src][:, :].rearrange("p (c n) -> p c n", c=DC),
                                          xT_hi[:, :, dst].bitcast(F32), ALU.subtract).then_inc(norm[n]["lo"], 2)
                return stage

            def row_eps(n):
                def stage(b):
                    dve.wait_ge(norm[n]["aggr"], b + 1)
                    dve.tensor_scalar(ve[:, b:b + 1], mv[:, b, 1:2], LN_EPS, None, ALU.add)\
                        .then_inc(norm[n]["var"], 1)
                return stage

            def stepper(layer):
                done = [0]

                def step(ins):
                    done[0] += 1
                    ins.then_inc(rout[layer]["step"], 1)
                    dve.wait_ge(rout[layer]["step"], done[0])
                return step

            steps_of = [stepper(0), stepper(1)]

            def wide(v):
                return v.unsqueeze(2).to_broadcast([P, PER, NE])

            def router_logits(layer):
                s, step = rout[layer], steps_of[layer]

                def stage(b):
                    if not last_of_block(b):
                        return
                    g = b // PER
                    dve.wait_ge(s["logits"], g + 1)
                    if g >= 1:
                        dve.wait_ge(s["exp"], (1 + layer) * g)
                    lg = bank[LOGITS_BANK[layer]][:, 128:128 + PER * 2 * NL].rearrange("p (b e) -> p b e", b=PER)
                    if layer == 0:
                        ins = dve.tensor_tensor(z[:, :, 0:NE], lg[:, :, 0:NE],
                                                rb[:].unsqueeze(1).to_broadcast([P, PER, NE]), ALU.add)
                    else:
                        ins = dve.tensor_copy(z[:], lg[:, :, 0:NCW])
                    step(ins)
                    n = (NE, NCW)[layer]
                    dve.tensor_tensor(z[:, :, 0:n], z[:, :, 0:n], lg[:, :, NL:NL + n], ALU.add)\
                        .then_inc(s["z"], 1)
                    dve.wait_ge(s["z"], g + 1)
                    step(dve.tensor_reduce(rowst[:], z[:, :, 0:NE], AX_X, ALU.max))
                    dve.tensor_tensor(z[:, :, 0:NE], z[:, :, 0:NE], wide(rowst[:]), ALU.subtract)\
                        .then_inc(s["centred"], 1)
                return stage

            def router_probs(layer):
                s, step = rout[layer], steps_of[layer]

                def stage(b):
                    if not last_of_block(b):
                        return
                    dve.wait_ge(s["exp"], (1 + layer) * (b // PER + 1))
                    step(dve.tensor_reduce(rowst[:], ez[:], AX_X, ALU.add))
                    step(dve.reciprocal(rowrc[:], rowst[:]))
                    step(dve.tensor_tensor(probs[:, :, 0:NE], ez[:], wide(rowrc[:]), ALU.mult))
                return stage

            def router_top(layer):
                s, step = rout[layer], steps_of[layer]

                def stage(b):
                    if not last_of_block(b):
                        return
                    g = b // PER
                    for k in range(PER):
                        last = dve.max(top8[:, k, :], probs[:, k, 0:NE])
                    step(last)
                    step(dve.memset(top8[:, :, TOPK[layer]:8], -1.0))
                    for k in range(PER):
                        last = dve.match_replace(rest[:, k, :], top8[:, k, :], probs[:, k, :], 0.0)
                    step(last)
                    step(dve.tensor_tensor(rest[:, :, 0:NE], probs[:, :, 0:NE], rest[:, :, 0:NE], ALU.subtract))
                    step(dve.tensor_reduce(rowst[:], rest[:, :, 0:NE], AX_X, ALU.add))
                    if layer == 0:
                        step(dve.tensor_scalar(rowst[:], rowst[:], TOPK_EPS, None, ALU.add))
                    step(dve.reciprocal(rowrc[:], rowst[:]))
                    if g >= 1:
                        dve.wait_ge(s["cwT"], g)
                    if layer == 0:
                        dve.memset(cw[:, :, NE:NCW], 1.0)
                    else:
                        step(dve.tensor_scalar(es[:], es[:], 1.0, None, ALU.add))
                        dve.reciprocal(cw[:, :, NE], es[:])
                    dve.tensor_tensor(cw[:, :, 0:NE], rest[:, :, 0:NE], wide(rowrc[:]), ALU.mult)\
                        .then_inc(s["cw"], 1)
                return stage

            def split_tile(layer, t, slot):
                f = ffn[layer]
                dve.wait_ge(f["w_hi"], t + 1)
                dve.tensor_tensor(w_lo[:, slot, :], w_raw[:, slot, :], w_hi[:, slot, :].bitcast(F32),
                                  ALU.subtract).then_inc(f["w_lo"], 1)

            def add_sum(layer, downs, blk, opens=False):
                f = ffn[layer]
                dve.wait_ge(f["down"], downs)
                dst = accT[:, :, blk * BLK:blk * BLK + BLK]
                if opens:
                    if blk == 0 and layer == 0:
                        dve.wait_ge(a0["res"], NB)
                    elif blk == 0:
                        dve.wait_ge(ffn[0]["turned"], NB)
                    dve.tensor_copy(dst, pair_bank[:]).then_inc(f["summed"], 1)
                    return
                dve.tensor_tensor(dst, pair_bank[:], dst, ALU.add).then_inc(f["summed"], 1)

            def hidden(layer, n, par, first, comb_at, comb_count):
                f = ffn[layer]
                dve.wait_ge(f["silu"], n + 1)
                dve.wait_ge(f["u"], n + 1)
                if not (isinstance(n, int) and n == 0):
                    dve.wait_ge(f["h"], n)
                dve.tensor_tensor(gu[:], sg[:, par, :], bank[2 + ffn_bank(n, par)][:, :], ALU.mult)\
                    .then_inc(f["gu"], 1)
                dve.wait_ge(f["gu"], n + 1)
                dve.wait_ge(comb_ok[layer][comb_at[0]], comb_count)
                if not first:
                    dve.wait_ge(f["h_lo"], n - 1)
                dve.tensor_tensor(hh[:, par, :], gu[:], comb[:, comb_at[0], comb_at[1], :], ALU.mult)\
                    .then_inc(f["h"], 1)

            def hidden_low(layer, n, par):
                f = ffn[layer]
                dve.wait_ge(f["h_hi"], n + 1)
                dve.tensor_tensor(h_lo[:, par, :], hh[:, par, :], h_hi[:, par, :].bitcast(F32),
                                  ALU.subtract).then_inc(f["h_lo"], 1)

            def first_hidden(layer, k):
                blk, slot, opening = first_round(k)
                hidden(layer, k, k % 2, k < 2, (blk, k % 2), 32 if opening else 64)

            def first_sum_and_low(layer, k):
                if k >= 2 and k % 2 == 0:
                    u = k // 2 - 1
                    add_sum(layer, k, u // 2, opens=u % 2 == 0)
                hidden_low(layer, k, k % 2)

            def add_ffn(layer, src):
                def stage(k):
                    f = ffn[layer]
                    dve.wait_ge(f["turned"], k // 2 * 2 + 2 if layer == 0 else k + 1)
                    o = k % 2 * D if layer == 0 else 0
                    dve.scalar_tensor_tensor(x[:, k, :], bank[src(k)][:, o:o + D], tg[:, 2 + layer:3 + layer],
                                             x[:, k, :], ALU.mult, ALU.add).then_inc(f["x"], 1)
                return stage

            def early_split(layer):
                def stage(t):
                    if t < SLOTS:
                        split_tile(layer, t, t)
                return stage

            def early(part, layer):
                def stage(k):
                    if k < EARLY - 1:
                        part(layer, k)
                return stage

            def maxes(b):
                dve.wait_ge(a0["sc"], b + 1)
                if b >= 2:
                    dve.wait_ge(a0["exp"], 2 * (b - 1))
                dve.tensor_reduce(nmx[:, b % 2, :], bank[A_SCORES][:, :].rearrange("p (c s) -> p c s", c=2), AX_X,
                                  ALU.max, negate=True).then_inc(a0["max"], 1)

            def sums(b):
                dve.wait_ge(a0["exp"], 2 * (b + 1))
                dve.reciprocal(rr[:, b % 2, :], rs[:, b % 4, :]).then_inc(a0["rec"], 1)

            def weigh_out(b):
                dve.wait_ge(a0["txT"], b + 1)
                dve.wait_ge(a0["rec"], b + 1)
                if b >= 2:
                    dve.wait_ge(a0["tx"], b - 1)
                dve.tensor_tensor(txT[b % 2].rearrange("p (c l) -> p c l", c=2),
                                  bank[A_TX][:, 0:2 * LAT].rearrange("p (c l) -> p c l", c=2),
                                  rr[:, b % 2, :].unsqueeze(2).to_broadcast([P, 2, LAT]), ALU.mult)\
                    .then_inc(a0["txT_sb"], 1)

            def tx_stats(b):
                dve.wait_ge(a0["tx_sb"], b + 1)
                dve.bn_stats(tx6[:, b % 2, :], tx[b % 4]).then_inc(a0["st"], 1)

            def tx_aggregate(b):
                dve.wait_ge(a0["st"], b + 1)
                if b >= 2:
                    dve.wait_ge(a0["means"], b - 1)
                dve.bn_aggr(txmv[:, b % 2, :], tx6[:, b % 2, :]).then_inc(a0["ag"], 1)

            def tx_mean(b):
                dve.wait_ge(a0["means"], b + 1)
                dve.tensor_copy(mu[:, b % 4, :], bank[A_MEANS][0:LAT, 0:1]).then_inc(a0["mu"], 1)

            def tx_deviation(b):
                dve.wait_ge(a0["mu"], b + 1)
                dve.tensor_tensor(dmu[:, b % 2, :], txmv[:, b % 2, 0:1], mu[:, b % 4, :], ALU.subtract)\
                    .then_inc(a0["d"], 1)

            def tx_square(b):
                dve.wait_ge(a0["d"], b + 1)
                if b >= 2:
                    dve.wait_ge(a0["means"], b)
                dve.scalar_tensor_tensor(q2[:, b % 2, :], dmu[:, b % 2, :], dmu[:, b % 2, :],
                                         txmv[:, b % 2, 1:2], ALU.mult, ALU.add).then_inc(a0["q"], 1)

            def tx_var(b):
                dve.wait_ge(a0["means"], b + 2)
                if b >= 2:
                    dve.wait_ge(a0["rstd"], b - 1)
                dve.tensor_scalar(hve[:, b % 2, :], bank[A_MEANS][0:LAT, 1:2], LN_EPS, None, ALU.add)\
                    .then_inc(a0["var"], 1)

            def tx_centred(b):
                dve.wait_ge(a0["mu"], b + 1)
                dve.scalar_tensor_tensor(hu[b % 2], tx[b % 4], mu[:, b % 4, :], lnorm[:, 0, :],
                                         ALU.subtract, ALU.mult).then_inc(a0["u"], 1)

            def tx_scaled(b):
                dve.wait_ge(a0["rstd"], b + 1)
                dve.wait_ge(a0["u"], b + 1)
                if b >= 2:
                    dve.wait_ge(a0["h"], b - 1)
                dve.scalar_tensor_tensor(hv[b % 2], hu[b % 2], hrstd[:, b % 2, :], lnorm[:, 1, :],
                                         ALU.mult, ALU.add).then_inc(a0["v"], 1)

            def lat_add(b):
                dve.wait_ge(a0["w"], b + 1)
                dve.wait_ge(a0["res"], b + 1)
                dve.scalar_tensor_tensor(x[:, b, :], bank[A_OUT][:, 0:D], tg[:, 0:1], x[:, b, :],
                                         ALU.mult, ALU.add).then_inc(a0["x"], 1)

            run(A_STEPS,
                (SCORES, maxes), (WEIGH, weigh_out), (MEAN, tx_mean), (VAR, tx_var), (MEAN, tx_deviation),
                (VAR, tx_centred), (MEAN, tx_square), (A_FFN + 1, early(first_hidden, 0)),
                (LOGITS + 1, router_top(0)), (TURN_X, split_rows(1, lambda k: A_TX)), (VAR, tx_scaled),
                (LOGITS, router_logits(0)), (OUT, lat_add),
                (LOAD, two(row_stats(0, lambda b: dve.wait_ge(x_in_ok[b // PER], 16)))), (TURN_TX, tx_stats),
                (LOAD, two(row_aggregate(0))), (STATS, row_stats(1, lambda b: dve.wait_ge(a0["x"], b + 1))),
                (TURN_TX, tx_aggregate), (NORM, two(normalise(0))), (LOAD, two(row_eps(0))),
                (STATS, row_aggregate(1)), (SCORES, sums), (STATS, row_eps(1)), (XN, normalise(1)),
                (LOGITS, router_probs(0)), (A_SPLIT, early_split(0)), (A_FFN + 1, early(first_sum_and_low, 0)))

            def experts(layer):
                n_round, left = rounds_of(layer)
                for k in range(EARLY - 1, FIRST):
                    first_hidden(layer, k)
                    first_sum_and_low(layer, k)
                    if layer == 0 and k in QKV_STEPS:
                        a = QKV_STEPS.index(k) * DC * D
                        dve.wait_ge(qkv_hi_ok, QKV_STEPS.index(k) + 1)
                        dve.tensor_tensor(qkv_lo[:, a:a + DC * D], qkv_raw[:, a:a + DC * D],
                                          qkv_hi[:, a:a + DC * D].bitcast(F32), ALU.subtract).then_inc(qkv_lo_ok, 1)
                    if k >= FIRST - 2:
                        split_tile(layer, SLOTS + k % 2, k % 2)

                def body(i, last):
                    for q in range(2):
                        for m in range(2 * NBLK):
                            k = q * 2 * NBLK + m
                            n = i * FIRST + k
                            hidden(layer, n, m % 2, False, (m // 2, m % 2), i * 64 + (q + 1) * 32)
                            if m % 2 == 0:
                                add_sum(layer, n, (m // 2 - 1) % NBLK)
                            hidden_low(layer, n, m % 2)
                            if last and layer == 1:
                                for b in final_batches(k - 1):
                                    add_ffn(1, lambda k: 4 + k % 2)(b)
                            if m in (3, 5):
                                slot = (2 * q + 2 + (m == 5)) % SLOTS
                                if q == 0:
                                    split_tile(layer, i * SLOTS + slot, slot)
                                elif not last or slot < left:
                                    split_tile(layer, i * SLOTS + SLOTS + slot, slot)

                with dve.Fori(1, n_round - 1) as i:
                    body(i, False)
                body(n_round - 1, True)
                steps = n_round * 4 * NBLK
                for m in range(left * NBLK):
                    hidden(layer, steps + m, m % 2, False, (m, 0), n_round * 64 + 16)
                    add_sum(layer, steps + m, (m - 1) % NBLK)
                    hidden_low(layer, steps + m, m % 2)
                add_sum(layer, steps + left * NBLK, NBLK - 1)

            experts(0)

            dve.wait_ge(later_ok, 16 * 4)

            def masked(b):
                dve.wait_ge(a1["sc"], b + 1)
                if b >= 2:
                    dve.wait_ge(a1["exp"], b - 1)
                dve.scalar_tensor_tensor(sm[b % 2], bank[B_SC][:, 0:P], float(D) ** -0.5, mask[:, b, :],
                                         ALU.mult, ALU.add).then_inc(a1["sm"], 1)

            def masked_max(b):
                dve.wait_ge(a1["sm"], b + 1)
                dve.tensor_reduce(nmx1[:, b % 2, :], sm[b % 2], AX_X, ALU.max, negate=True).then_inc(a1["max"], 1)

            def att_scale(b):
                dve.wait_ge(a1["exp"], b + 1)
                dve.reciprocal(rr1[:, b % 2, :], rs1[:, b % 4, :]).then_inc(a1["rec"], 1)
                dve.wait_ge(a1["rec"], b + 1)
                dve.tensor_scalar(rt1[:, b % 2, :], rr1[:, b % 2, :], tg[:, 1:2], None, ALU.mult)\
                    .then_inc(a1["rt"], 1)

            def att_add(b):
                dve.wait_ge(a1["rt"], b + 1)
                dve.wait_ge(a1["o"], b + 1)
                dve.wait_ge(a1["res"], b + 1)
                dve.scalar_tensor_tensor(x[:, b, :], bank[B_O][:, 0:D], rt1[:, b % 2, :], x[:, b, :],
                                         ALU.mult, ALU.add).then_inc(a1["x"], 1)

            run(B_STEPS,
                (B_FFN + 1, early(first_hidden, 1)), (B_OUT, att_add), (B_SUMS, two(add_ffn(0, lambda k: B_SUM))),
                (B_SCORES, masked), (B_OUT, row_stats(3, lambda b: dve.wait_ge(a1["x"], b + 1))),
                (B_SUMS, two(row_stats(2, lambda b: dve.wait_ge(ffn[0]["x"], b + 1)))),
                (B_LOGITS + 1, router_top(1)), (B_SCORES, masked_max), (B_XN, two(normalise(2))),
                (B_XN3, normalise(3)), (B_OUT, row_aggregate(3)), (B_SUMS, two(row_aggregate(2))),
                (B_OUT, row_eps(3)), (B_SUMS, two(row_eps(2))), (B_TURN, split_pair(2, B_ROWS)),
                (B_TURN_P, att_scale), (B_LOGITS, router_logits(1)), (B_TURN3, split_rows(3, rows3_bank)),
                (B_LOGITS, router_probs(1)), (B_SPLIT, early_split(1)), (B_FFN + 1, early(first_sum_and_low, 1)))
            experts(1)
            for k in final_batches(FIRST - 1) + final_batches(FIRST):
                add_ffn(1, lambda k: 4 + k % 2)(k)

        @block.tensor
        def _(pe):
            def mm3(dst, w, xv, start=True, stop=True):
                pe.matmul(dst, w[0], xv[0], start=start, stop=False)
                pe.matmul(dst, w[0], xv[1], start=False, stop=False)
                return pe.matmul(dst, w[1], xv[0], start=False, stop=stop)

            def mm3c(dst, ws, xs):
                for c in range(len(ws)):
                    last = mm3(dst, ws[c], xs[c], start=c == 0, stop=c == len(ws) - 1)
                return last

            def xT(c, a, b):
                return (xT_hi[:, c, a:b], xT_lo[:, c, a:b])

            def turn_rows(n, dst, bank_free):
                def stage(k):
                    s = norm[n]
                    pe.wait_ge(s["xn"], k + 1)
                    if k >= 1:
                        pe.wait_ge(s["lo"], k)
                    bank_free(k)
                    for c in range(DC):
                        last = pe.transpose(bank[dst(k)][:, c * P:c * P + P], xn[:, k, c * P:c * P + P], ident[:])
                    last.then_inc(s["xTp"], 1)
                return stage

            def turn_pair(n, dst):
                def stage(i):
                    if 2 * i < NB:
                        s = norm[n]
                        pe.wait_ge(s["xn"], 2 * i + 2)
                        if i >= 1:
                            pe.wait_ge(s["lo"], 2 * i)
                        for c in range(DC):
                            for j in range(2):
                                o = (2 * c + j) * P
                                last = pe.transpose(bank[dst][:, o:o + P],
                                                    xn[:, 2 * i + j, c * P:c * P + P], ident[:])
                        last.then_inc(s["xTp"], 2)
                return stage

            def turn_sums(layer, k, dst, o=0):
                for c in range(DC):
                    last = pe.transpose(bank[dst][:, o + c * P:o + c * P + P], accT[:, c, k * P:k * P + P], ident[:])
                last.then_inc(ffn[layer]["turned"], 1)

            def logits(layer, bank_free):
                def stage(b):
                    s = rout[layer]
                    pe.wait_ge(norm[1 + 2 * layer]["lo"], b + 1)
                    if b % PER == 0 and b >= PER:
                        pe.wait_ge(s["z"], b // PER)
                    bank_free(b)
                    dst = bank[LOGITS_BANK[layer]]
                    o = 128 + b % PER * 2 * NL
                    for c in range(DC):
                        hi, lo = xT(c, b * P, b * P + P)
                        w = rw[:, layer * DC + c, :, :]
                        pe.matmul(dst[:, o:o + 2 * NL], hi, w.rearrange("p h n -> p (h n)"), start=c == 0, stop=False)
                        last = pe.matmul(dst[:, o:o + NL], lo, w[:, 0, :], start=False, stop=c == DC - 1)
                    if last_of_block(b):
                        last.then_inc(s["logits"], 1)
                return stage

            def turn_weights(layer, bank_free):
                def stage(b):
                    if not last_of_block(b):
                        return
                    s = rout[layer]
                    pe.wait_ge(s["cw"], b // PER + 1)
                    bank_free(b)
                    for k in range(PER):
                        last = pe.transpose(bank[CW_BANK[layer]][0:NCW, k * P:k * P + P], cw[:, k, :], ident[:])
                    last.then_inc(s["cwT"], 1)
                return stage

            def blocks_before(step, lag):
                return max(0, min(NBLK, (step - lag) // PER))

            def gate_up(layer, n, blk, slot, par, first, tile):
                f = ffn[layer]
                if tile is not None:
                    pe.wait_ge(f["w_lo"], tile + 1)
                x4 = [xT(c, blk * BLK, blk * BLK + BLK) for c in range(DC)]
                early = isinstance(n, int) and n < EARLY
                if not first:
                    pe.wait_ge(f["silu"], n if early else n - 1)
                mm3c(bank[ffn_bank(n, par)][:, :], [(w_hi[:, slot, c * P:c * P + P], w_lo[:, slot, c * P:c * P + P])
                                       for c in range(DC)], x4).then_inc(f["g"], 1)
                if not first:
                    pe.wait_ge(f["gu"], n if early else n - 1)
                mm3c(bank[2 + ffn_bank(n, par)][:, :], [(w_hi[:, slot, (DC + c) * P:(DC + c) * P + P],
                                            w_lo[:, slot, (DC + c) * P:(DC + c) * P + P])
                                           for c in range(DC)], x4).then_inc(f["u"], 1)

            def down(layer, n, slot, par, opens, closes, unit, first):
                f = ffn[layer]
                pe.wait_ge(f["h_lo"], n + 1)
                if opens and not first:
                    pe.wait_ge(f["summed"], unit)
                for c in range(DC):
                    a = WGU + c * P
                    last = mm3(pair_bank[:, c, :], (w_hi[:, slot, a:a + P], w_lo[:, slot, a:a + P]),
                               (h_hi[:, par, :], h_lo[:, par, :]), start=opens, stop=closes)
                last.then_inc(f["down"], 1)

            def first_gate_up(layer, k):
                blk, slot, _ = first_round(k)
                gate_up(layer, k, blk, slot, k % 2, k == 0, slot if k < SLOTS else None)

            def first_down(layer, k):
                down(layer, k, k % SLOTS, k % 2, k % 2 == 0, k % 2 == 1, k // 2, k == 0)

            def final_rows(k):
                units = TILES[1] // 2 * NBLK
                pe.wait_ge(ffn[1]["summed"], units - NBLK + k // PER + 1)
                if k >= 2:
                    pe.wait_ge(ffn[1]["x"], k - 1)
                turn_sums(1, k, 4 + k % 2)

            def early_ffn(layer, banks_free):
                def stage(k):
                    if k < EARLY:
                        if k == 0:
                            banks_free()
                        first_gate_up(layer, k)
                return stage

            def early_down(layer):
                def stage(k):
                    if k < EARLY - 2:
                        first_down(layer, k)
                return stage

            def latents(b):
                pe.wait_ge(norm[0]["xn"], b + 1)
                if b % PER == 0:
                    pe.wait_ge(ctx_ok[b // PER], 16)
                if b >= 1:
                    pe.wait_ge(a0["thph_sb"], 2 * b)
                    pe.wait_ge(a0["g_sb"], b)
                pe.matmul(bank[A_THPH][0:LAT, 0:D], lw[:, 0, :], ctx_sb[:, b, :], start=True, stop=True)
                pe.matmul(bank[A_THPH][0:LAT, D:2 * D], lw[:, 1, :], xn[:, b, :], start=True, stop=True)
                for c in range(2):
                    last = pe.matmul(bank[A_G][:, c * LAT:c * LAT + LAT], xn[:, b, c * P:c * P + P], lw[:, 2, :],
                                     start=True, stop=True)
                last.then_inc(a0["thph"], 1)

            def scores(b):
                pe.wait_ge(a0["thph_sb"], 2 * (b + 1))
                if b >= 1:
                    pe.wait_ge(a0["exp"], 2 * b)
                for c in range(2):
                    last = pe.matmul(bank[A_SCORES][:, c * D:c * D + D], thph[b % 2][:, 0, c * P:c * P + P],
                                     thph[b % 2][:, 1, :], start=True, stop=True)
                last.then_inc(a0["sc"], 1)

            def turn_p(b):
                pe.wait_ge(a0["exp"], 2 * (b + 1))
                if b >= 1:
                    pe.wait_ge(a0["pT_sb"], b)
                for j in range(2):
                    for c in range(2):
                        last = pe.transpose(bank[A_P][:, j * D + c * P:j * D + c * P + P],
                                            p_sb[b % 2][:, c, j * P:j * P + P], ident[:])
                last.then_inc(a0["pT"], 1)

            def weigh(b):
                pe.wait_ge(a0["pT_sb"], b + 1)
                pe.wait_ge(a0["g_sb"], b + 1)
                if b >= 1:
                    pe.wait_ge(a0["txT_sb"], b)
                if b + WEIGH - TURN_X >= 1:
                    pe.wait_ge(norm[1]["lo"], b + WEIGH - TURN_X)
                for c in range(2):
                    for j in range(2):
                        last = pe.matmul(bank[A_TX][:, c * LAT:c * LAT + LAT],
                                         pT_sb[b % 2][:, j * D + c * P:j * D + c * P + P],
                                         g_sb[b % 4][:, j * LAT:j * LAT + LAT], start=j == 0, stop=j == 1)
                last.then_inc(a0["txT"], 1)

            def turn_tx(b):
                pe.wait_ge(a0["txT_sb"], b + 1)
                if b >= 1:
                    pe.wait_ge(a0["tx_sb"], b)
                if turned := blocks_before(b + TURN_TX, TURN_CW):
                    pe.wait_ge(rout[0]["turned"], turned)
                for c in range(2):
                    last = pe.transpose(bank[A_TURNTX][0:LAT, c * P:c * P + P], txT[b % 2][:, c * LAT:c * LAT + LAT],
                                        ident[:])
                last.then_inc(a0["tx"], 1)

            def means(b):
                if b >= 1:
                    pe.wait_ge(a0["q"], b)
                    pe.wait_ge(a0["mu"], b)
                if b >= 2:
                    pe.wait_ge(a0["var"], b - 1)
                if read := blocks_before(b + MEAN, LOGITS):
                    pe.wait_ge(rout[0]["z"], read)
                if b < NB:
                    pe.wait_ge(a0["ag"], b + 1)
                if b >= 1:
                    last = pe.matmul(bank[A_MEANS][0:LAT, 1:2], ones[:], q2[:, (b - 1) % 2, :], start=True, stop=True)
                if b < NB:
                    last = pe.matmul(bank[A_MEANS][0:LAT, 0:1], ones[:], txmv[:, b % 2, 0:1], start=True, stop=True)
                last.then_inc(a0["means"], 1)

            def last_means(b):
                if b == NB - 1:
                    means(NB)

            def lat_out(b):
                pe.wait_ge(a0["h"], b + 1)
                if b >= 1:
                    pe.wait_ge(a0["x"], b)
                pe.matmul(bank[A_OUT][:, 0:D], low[:], hr[b % 2], start=True, stop=True).then_inc(a0["w"], 1)

            def rows_bank_free(k):
                pe.wait_ge(a0["txT_sb"], min(k + TURN_X - WEIGH + 1, NB))

            def logits_bank_free(b):
                pe.wait_ge(a0["var"], min(b + LOGITS - MEAN, NB))
                pe.wait_ge(a0["mu"], min(b + LOGITS - MEAN + 1, NB))

            def weights_bank_free(b):
                pe.wait_ge(a0["tx_sb"], min(b + TURN_CW - TURN_TX + 1, NB))

            pe.wait_ge(small_ok, 16 * N_SMALL)
            pe.wait_ge(const_ok, 3)
            pe.wait_ge(rw_lo_ok, 1)

            def early_banks_free0():
                pe.wait_ge(a0["thph_sb"], 2 * NB)
                pe.wait_ge(a0["g_sb"], NB)
                pe.wait_ge(a0["exp"], 2 * NB)
                pe.wait_ge(a0["pT_sb"], NB)

            run(A_STEPS,
                (SCORES, scores), (TURN_P, turn_p), (MEAN, means), (MEAN + 1, last_means), (WEIGH, weigh),
                (TURN_TX, turn_tx), (TURN_X, turn_rows(1, lambda k: A_TX, rows_bank_free)), (LATENTS, latents),
                (TURN_CW, turn_weights(0, weights_bank_free)), (OUT, lat_out),
                (LOGITS, logits(0, logits_bank_free)), (A_FFN + 2, early_down(0)),
                (A_FFN, early_ffn(0, early_banks_free0)))

            def experts(layer):
                n_round, left = rounds_of(layer)
                first_down(layer, EARLY - 2)
                for k in range(EARLY - 1, FIRST):
                    if k + 1 < FIRST:
                        first_gate_up(layer, k + 1)
                    else:
                        gate_up(layer, FIRST, 0, 0, 0, False, SLOTS)
                    first_down(layer, k)

                def body(i, last):
                    for k in range(FIRST):
                        n = i * FIRST + k
                        q, m = (k + 1) // (2 * NBLK), (k + 1) % (2 * NBLK)
                        if q < 2:
                            slot = 2 * q + m % 2
                            gate_up(layer, n + 1, m // 2, slot, m % 2, False,
                                    i * SLOTS + slot if m < 2 else None)
                        elif not last or left:
                            gate_up(layer, n + 1, 0, 0, 0, False, i * SLOTS + SLOTS)
                        q, m = k // (2 * NBLK), k % (2 * NBLK)
                        down(layer, n, 2 * q + m % 2, k % 2, m % 2 == 0, m % 2 == 1,
                             i * 2 * NBLK + k // 2, False)
                        if last and layer == 1:
                            for b in final_batches(k):
                                final_rows(b)

                with pe.Fori(1, n_round - 1) as i:
                    body(i, False)
                body(n_round - 1, True)
                for m in range(left * NBLK):
                    n = n_round * 4 * NBLK + m
                    if m + 1 < left * NBLK:
                        gate_up(layer, n + 1, m + 1, 0, (m + 1) % 2, False, None)
                    down(layer, n, 0, m % 2, True, True, n_round * 2 * NBLK + m, False)
                return n_round * 2 * NBLK + left * NBLK

            pe.wait_ge(norm[1]["lo"], NB)
            pe.wait_ge(rout[0]["turned"], NBLK)
            units = experts(0)

            def wqkv(j, c, a, b):
                o = (j * DC + c) * D
                return (qkv_hi[:, o + a:o + b], qkv_lo[:, o + a:o + b])

            def sums_to_rows(i):
                if 2 * i < NB:
                    pe.wait_ge(ffn[0]["summed"], units)
                    if i >= 1:
                        pe.wait_ge(ffn[0]["x"], 2 * i)
                    for k in (2 * i, 2 * i + 1):
                        turn_sums(0, k, B_SUM, k % 2 * D)

            def project(b):
                B, j = b // PER, b % PER
                pe.wait_ge(norm[2]["lo"], PER * B + PER)
                if b >= 1:
                    pe.wait_ge(a1["proj_sb"], b)
                a = j % DC * P
                mm3c(bank[B_PROJECT][:, :], [wqkv(j // DC, c, a, a + P) for c in range(DC)],
                     [xT(c, B * BLK, B * BLK + BLK) for c in range(DC)]).then_inc(a1["proj"], 1)

            def values(b):
                if b >= 1:
                    pe.wait_ge(a1["v_sb"], b)
                if turned := blocks_before(b + B_SCORES, B_TURN_CW):
                    pe.wait_ge(rout[1]["turned"], turned)
                mm3c(bank[B_V][:, 0:D], [xT(c, b * P, b * P + P) for c in range(DC)],
                     [wqkv(2, c, 0, D) for c in range(DC)]).then_inc(a1["v"], 1)

            def scores1(b):
                B, o = b // PER, b % PER * P
                pe.wait_ge(a1["proj_sb"], PER * (B + 1))
                if b >= 1:
                    pe.wait_ge(a1["sm"], b)
                for c in range(DC):
                    last = pe.matmul(bank[B_SC][:, 0:P], QT[B % 2][:, c, o:o + P], KT[B % 2][:, c, o:o + P],
                                     start=c == 0, stop=c == DC - 1)
                last.then_inc(a1["sc"], 1)

            def turn_p1(b):
                step = b + B_TURN_P
                pe.wait_ge(a1["exp"], b + 1)
                if b >= 1:
                    pe.wait_ge(a1["pT_sb"], b)
                if read := blocks_before(step, B_LOGITS):
                    pe.wait_ge(rout[1]["z"], read)
                pe.transpose(bank[B_P][:, 0:P], pr[b % 2], ident[:]).then_inc(a1["pT"], 1)

            def weigh1(b):
                pe.wait_ge(a1["pT_sb"], b + 1)
                pe.wait_ge(a1["v_sb"], b + 1)
                if b >= 1:
                    pe.wait_ge(a1["x"], b)
                if (turned := b + B_OUT - B_TURN3) >= 1 and rows3_bank(turned - 1) == B_O:
                    pe.wait_ge(norm[3]["lo"], turned)
                pe.matmul(bank[B_O][:, 0:D], prT[b % 2], V_sb[b % 4], start=True, stop=True).then_inc(a1["o"], 1)

            def logits1_bank_free(b):
                pe.wait_ge(a1["pT_sb"], min(b + B_LOGITS - B_TURN_P + 1, NB))

            def weights1_bank_free(b):
                pe.wait_ge(a1["v_sb"], min(b + B_TURN_CW - B_SCORES + 1, NB))

            pe.wait_ge(qkv_lo_ok, len(QKV_STEPS))

            def rows3_bank_free(k):
                if rows3_bank(k) == B_O:
                    pe.wait_ge(a1["x"], min(k + B_TURN3 - B_OUT + 1, NB))

            def early_banks_free1():
                pe.wait_ge(ffn[0]["x"], NB)
                pe.wait_ge(norm[2]["lo"], NB)
                pe.wait_ge(a1["proj_sb"], NB)
                pe.wait_ge(norm[3]["lo"], B_FFN - B_TURN3)

            run(B_STEPS,
                (B_OUT, weigh1), (B_SUMS, sums_to_rows), (B_SCORES, scores1), (B_TURN_P, turn_p1),
                (B_TURN, turn_pair(2, B_ROWS)), (B_PROJ, project), (B_SCORES, values), (B_FFN + 2, early_down(1)),
                (B_TURN3, turn_rows(3, rows3_bank, rows3_bank_free)), (B_LOGITS, logits(1, logits1_bank_free)),
                (B_TURN_CW, turn_weights(1, weights1_bank_free)), (B_FFN, early_ffn(1, early_banks_free1)))

            pe.wait_ge(rout[1]["turned"], NBLK)
            pe.wait_ge(a1["sm"], NB)
            experts(1)
            for k in final_batches(FIRST):
                final_rows(k)


def _tiles(gate, up, down, np):
    n = gate.shape[0] // P

    def turned(w):
        return w.reshape(n, P, DC, P).transpose(0, 3, 2, 1).reshape(n, P, DC * P)

    return np.ascontiguousarray(np.concatenate([turned(gate), turned(up), down.reshape(n, P, D)], axis=2))


def kernel(**inputs):
    import numpy as np
    import concourse.bacc as _bacc
    from concourse import mybir as _mybir
    from concourse.bass_utils import run_bass_kernel_spmd as _run

    a = {k: np.asarray(v) for k, v in inputs.items()}
    c = np.ascontiguousarray

    def wide(v):
        return c(np.broadcast_to(v.reshape(1, -1), (P, v.size)))

    def chunks(w):
        return w.T.reshape(DC, P, -1).transpose(1, 0, 2)

    def router_cols(w):
        return np.concatenate([w, np.zeros((NL - w.shape[0], D), w.dtype)])

    g0 = np.concatenate([a["L0_ffn_Wg"].transpose(0, 2, 1).reshape(-1, D), a["L0_ffn_sWg"].T])
    u0 = np.concatenate([a["L0_ffn_Wu"].transpose(0, 2, 1).reshape(-1, D), a["L0_ffn_sWu"].T])
    d0 = np.concatenate([a["L0_ffn_Wd"].reshape(-1, D), a["L0_ffn_sWd"]])
    egu, sgu = a["L1_ffn_expert_gate_up"], a["L1_ffn_shared_gate_up"]
    I, SI = egu.shape[1] // 2, sgu.shape[0] // 2
    pad = np.zeros((TILES[1] * P - NE * I - SI, D), egu.dtype)
    g1 = np.concatenate([egu[:, :I].reshape(-1, D), sgu[:SI], pad])
    u1 = np.concatenate([egu[:, I:].reshape(-1, D), sgu[SI:], pad])
    d1 = np.concatenate([a["L1_ffn_expert_down"].transpose(0, 2, 1).reshape(-1, D), a["L1_ffn_shared_down"].T, pad])
    arrays = {
        "x_in": c(a["x"]),
        "ctx_in": c(a["ctx_2048"]),
        "mask_in": c(a["mask_BxSxS2_ff0"]),
        "gates_in": wide(np.concatenate([a["g_xattn"], a["g_ffn"]])),
        "ident_in": np.eye(P, dtype=np.float32),
        "lat_w": c(np.stack([a["L0_xattn_theta_w"].T, a["L0_xattn_phi_w"].T, a["L0_xattn_g_w"].T], axis=1)),
        "lat_b": c(np.stack([a["L0_xattn_theta_b"], a["L0_xattn_phi_b"], a["L0_xattn_g_b"]], axis=1)),
        "lat_out_w": c(a["L0_xattn_out_w"].T),
        "lat_out_b": c(a["L0_xattn_out_b"].reshape(P, 1)),
        "lat_norm": c(np.stack([a["L0_xattn_ln_gamma"], a["L0_xattn_ln_beta"]], axis=1)),
        "qkv_w": c(np.stack([chunks(a[f"L1_xattn_W{n}"]) for n in "qkv"], axis=1).reshape(P, -1)),
        "qk_b": c(np.stack([a[f"L1_xattn_b{n}"].reshape(DC, P).T for n in "qk"], axis=1)),
        "v_b": wide(a["L1_xattn_bv"]),
        "router_w": c(np.stack([chunks(router_cols(a["L0_ffn_Wr"])).reshape(P, -1),
                                chunks(router_cols(np.concatenate([a["L1_ffn_gate_w"],
                                                                   a["L1_ffn_shared_gate_vec"]]))).reshape(P, -1)],
                               axis=1)),
        "router_b": wide(a["L0_ffn_bias"]),
        "ffn_w0": _tiles(g0, u0, d0, np),
        "ffn_w1": _tiles(g1, u1, d1, np),
    }
    nc = _bacc.Bacc("TRN2", target_bir_lowering=False, num_devices=1)
    ap = {n: nc.dram_tensor(n, v.shape, _mybir.dt.from_np(v.dtype), kind="ExternalInput").ap()
          for n, v in arrays.items()}
    out = nc.dram_tensor("out", (NB, P, D), _mybir.dt.float32, kind="ExternalOutput").ap()
    tiles = [ap.pop("ffn_w0"), ap.pop("ffn_w1")]
    gated_blocks(nc, out=out, ffn_w=tiles, **ap)
    r = _run(nc, [arrays], core_ids=[0])
    return r.results[0]["out"]
```
